# Optimizing a Trainium2 kernel written in Bass

```python
import numpy as np
import jax
import jax.numpy as jnp

def _softmax(x, axis=-1):
    return jax.nn.softmax(x, axis=axis)

def _gelu(x):
    return jax.nn.gelu(x, approximate=True)

def _silu(x):
    return jax.nn.silu(x)

def _sigmoid(x):
    return jax.nn.sigmoid(x)

def _layernorm(x, axis=-1, eps=1e-05):
    m = jnp.mean(x, axis=axis, keepdims=True)
    v = jnp.var(x, axis=axis, keepdims=True)
    return (x - m) / jnp.sqrt(v + eps)

def _scatter_add(tgt, idx, src, axis=0):
    return tgt.at[idx].add(src)

def _segment_sum(src, seg, n):
    return jax.ops.segment_sum(src, seg, n)
kernel_name = 'mk_seq_postln_d1_jaxref_r2_879bb4'

def setup_inputs(seed: int=0):
    np.random.seed(seed)
    _w = jnp.asarray

    def _L0_attn_setup():
        import jax, jax.numpy as jnp
        import numpy as np
        B, N, D_IN, D_OUT, HEADS = (4, 2048, 512, 512, 16)
        D_HEAD = D_OUT // HEADS
        key = jax.random.key(seed)
        ks = jax.random.split(key, 5)
        x = jax.random.normal(ks[0], (B, N, D_IN), dtype=jnp.float32)
        s_in = 1.0 / np.sqrt(D_IN)
        s_out = 1.0 / np.sqrt(D_OUT)
        Wq = jax.random.normal(ks[1], (D_IN, D_OUT), dtype=jnp.float32) * s_in
        Wk = jax.random.normal(ks[2], (D_IN, D_OUT), dtype=jnp.float32) * s_in
        Wv = jax.random.normal(ks[3], (D_IN, D_OUT), dtype=jnp.float32) * s_in
        Wo = jax.random.normal(ks[4], (D_OUT, D_OUT), dtype=jnp.float32) * s_out
        bo = jnp.zeros((D_OUT,), dtype=jnp.float32)
        return {'x': x, 'Wq': Wq, 'Wk': Wk, 'Wv': Wv, 'Wo': Wo, 'bo': bo}
    _L0_attn_in = _L0_attn_setup()

    def _L0_ffn_setup():
        import jax, jax.numpy as jnp
        import numpy as np
        INT4_QMAX = 7.0

        def simulate_quantize_int4(w):
            scale = jnp.max(jnp.abs(w)) / INT4_QMAX
            q = jnp.clip(jnp.round(w / scale), -8.0, 7.0)
            return q * scale
        key = jax.random.key(seed)
        k_x, k_w, k_bias, k_a, k_b = jax.random.split(key, 5)
        d_in, features, rank = (512, 512, 16)
        x = jax.random.normal(k_x, (4, 4096, d_in), dtype=jnp.float32)
        kernel = jax.random.normal(k_w, (d_in, features), dtype=jnp.float32)
        bias = jax.random.normal(k_bias, (features,), dtype=jnp.float32)
        a = jax.random.normal(k_a, (d_in, rank), dtype=jnp.float32) * (1.0 / np.sqrt(d_in))
        b = jax.random.normal(k_b, (rank, features), dtype=jnp.float32) * 0.01
        return {'x': x, 'kernel': kernel, 'bias': bias, 'a': a, 'b': b}
    _L0_ffn_in = _L0_ffn_setup()
    _d = {'L0_attn_x': _L0_attn_in['x'], 'L0_attn_Wq': _L0_attn_in['Wq'], 'L0_attn_Wk': _L0_attn_in['Wk'], 'L0_attn_Wv': _L0_attn_in['Wv'], 'L0_attn_Wo': _L0_attn_in['Wo'], 'L0_attn_bo': _L0_attn_in['bo'], 'L0_ffn_kernel': _L0_ffn_in['kernel'], 'L0_ffn_bias': _L0_ffn_in['bias'], 'L0_ffn_a': _L0_ffn_in['a'], 'L0_ffn_b': _L0_ffn_in['b']}
    _x0 = _d['L0_attn_x']
    _d['L0_attn_x'] = jax.random.normal(jax.random.fold_in(jax.random.key(seed), 1), (8, 2048, 512), dtype=_x0.dtype)
    del _x0
    return _d

def reference(L0_attn_x, L0_attn_Wq, L0_attn_Wk, L0_attn_Wv, L0_attn_Wo, L0_attn_bo, L0_ffn_kernel, L0_ffn_bias, L0_ffn_a, L0_ffn_b):

    def _L0_attn_ref(x, Wq, Wk, Wv, Wo, bo):
        import jax, jax.numpy as jnp
        import numpy as np
        B, N, D_IN, D_OUT, HEADS = (4, 2048, 512, 512, 16)
        D_HEAD = D_OUT // HEADS
        q = jax.nn.softmax(jnp.einsum('bni,io->bno', x, Wq), axis=-1)
        k = jax.nn.softmax(jnp.einsum('bni,io->bno', x, Wk), axis=-2)
        v = jnp.einsum('bni,io->bno', x, Wv)
        scale = 1.0 / np.sqrt(D_HEAD).astype(np.float32)
        ctx = jnp.einsum('bnd,bne->bde', k, v) * scale
        y = jnp.einsum('bnd,bde->bne', q, ctx) / jnp.float32(D_OUT)
        return jnp.einsum('bnd,de->bne', y, Wo) + bo

    def _L0_ffn_ref(x, kernel, bias, a, b):
        import jax, jax.numpy as jnp
        import numpy as np
        INT4_QMAX = 7.0

        def simulate_quantize_int4(w):
            scale = jnp.max(jnp.abs(w)) / INT4_QMAX
            q = jnp.clip(jnp.round(w / scale), -8.0, 7.0)
            return q * scale
        w = simulate_quantize_int4(kernel)
        y = jnp.einsum('bsd,df->bsf', x, w) + bias
        lora = jnp.einsum('bsr,rf->bsf', jnp.einsum('bsd,dr->bsr', x, a), b)
        return y + lora
    x = L0_attn_x
    x = _layernorm(x + _L0_attn_ref(x, L0_attn_Wq, L0_attn_Wk, L0_attn_Wv, L0_attn_Wo, L0_attn_bo), axis=-1)
    x = _layernorm(x + _L0_ffn_ref(x, L0_ffn_kernel, L0_ffn_bias, L0_ffn_a, L0_ffn_b), axis=-1)
    return x

_drawn_inputs = setup_inputs


def setup_inputs(seed=0):
    import zlib

    import numpy as np

    out = dict(_drawn_inputs(seed))
    spreads = {'L0_attn_bo': (0.0, 0.1)}
    factors = {'L0_attn_Wq': 33.814,
     'L0_attn_Wk': 33.866,
     'L0_attn_Wv': 33.827,
     'L0_attn_Wo': 33.709,
     'L0_ffn_a': 8.0,
     'L0_ffn_b': 8.0}
    for name, (base, spread) in spreads.items():
        noise = np.random.default_rng([zlib.crc32(name.encode()), seed]).standard_normal(out[name].shape)
        drawn = base * np.exp(spread * noise) if base else spread * noise
        out[name] = jnp.asarray(drawn.astype(out[name].dtype))
    for name, factor in factors.items():
        out[name] = (out[name] * factor).astype(out[name].dtype)
    return out
```

```python
import concourse.bass as bass
from concourse import mybir
from contextlib import ExitStack


P = 128
BATCHES, TOKENS, D = 8, 2048, 512
RANK = 16
CH = D // P
TILES = TOKENS // P
RING = 24
LEAD = 4
EPS = 1e-5
ATTN_SCALE = 1.0 / (D // 16) ** 0.5 / D
FAR = -3.0e38
PS = 4096.0
NS = 512.0
GS = 2.0 ** -22
TOP = 2.0 ** 13
ROT_STEPS = 9
ROT_A_STEPS = 5


def done(n):
    return n + 1 + LEAD


class Tile:

    def __init__(self, n, t, half, quad, q, ring, first=False):
        self.first = first
        self.n, self.t, self.half, self.quad, self.q, self.ring = n, t, half, quad, q, ring
        self.par = q % 2


def snapped(eng, value):
    return value if isinstance(value, int) else eng.snap(value)


def pair(eng, p, t, first=False):
    p = snapped(eng, p)
    n, ring = snapped(eng, p * 2), snapped(eng, p % (RING // 2) * 2)
    return [Tile(n + k, t + k, p, None, k, ring + k, first) for k in range(2)]


def quad(eng, p, t):
    p = snapped(eng, p)
    n, ring = snapped(eng, p * 4), snapped(eng, p % (RING // 4) * 4)
    return [Tile(n + k, t + k, p * 2 + k // 2, p, k, ring + k) for k in range(4)]


def walk(eng, do):

    def step(name, *args):
        if name in do:
            do[name](*args)

    step("setup")
    with eng.Fori(0, TILES // 4) as g:
        for x in quad(eng, g, g * 4):
            step("X", x)
    step("XS", 0)
    step("scale_a", 0)

    def alone(tiles, xs):
        for a, x in zip(tiles, xs):
            step("Sx", a)
            step("Tx", a)
            step("X", x)
            step("Lq", a)
            step("Lk", a)
            step("TP", a)

    alone(pair(eng, 0, 0, True), pair(eng, TILES // 2, 0))
    with eng.Fori(1, TILES // 2) as i:
        alone(pair(eng, i, i * 2, True), pair(eng, i + TILES // 2, i * 2))
    step("XS", 1)
    step("CT", 0)
    step("CB", 0)
    step("scale_b", 0)
    step("scale_a", 1)
    step("E0", 0)

    def period(b, last):

        def a_pair(i):
            return None if last else pair(eng, (b + 1) * (TILES // 2) + i, i * 2)

        def a_step(name, a):
            if not last:
                step(name, a)

        def b_unit(a, bs, xs):
            a_step("Sx", a)
            step("B", bs[0])
            a_step("Tx", a)
            a_step("X", xs[0])
            step("B", bs[1])
            a_step("Lq", a)
            a_step("Lk", a)
            a_step("X", xs[1])
            a_step("TP", a)

        with eng.Fori(0, 3) as g:
            a = a_pair(g) or [None, None]
            bs = quad(eng, b * 4 + g, g * 4)
            xs = [None] * 4 if last else quad(eng, (b + 2) * 4 + g, g * 4)
            b_unit(a[0], bs[0:2], xs[0:2])
            b_unit(a[1], bs[2:4], xs[2:4])
        a = a_pair(3) or [None, None]
        bs = quad(eng, b * 4 + 3, 12)
        xs = [None] * 4 if last else quad(eng, (b + 2) * 4 + 3, 12)
        for k in range(4):
            if k == 2:
                a_step("Sx", a[0])
            if k == 3:
                a_step("Tx", a[0])
            step("B", bs[k])
            a_step("X", xs[k])
        step("KS", b)
        step("GE", b)
        a_step("Lq", a[0])
        a_step("Lk", a[0])
        step("M", b, 0)
        a_step("TP", a[0])
        a_step("Sx", a[1])
        step("M", b, 1)
        a_step("Tx", a[1])
        step("M", b, 2)
        step("M", b, 3)
        a_step("XS", b + 2)
        a_step("Lq", a[1])
        a_step("Lk", a[1])
        cs = quad(eng, b * 4, 0)
        step("PM", cs[0])
        a_step("TP", a[1])

        def c_unit(a, c0, c1, c2, end):
            a_step("Sx", a)
            a_step("Tx", a)
            step("PM", c1)
            step("N1", c0)
            a_step("Lq", a)
            step("T1", c0)
            a_step("Lk", a)
            step("N1", c1)
            step("F", c0)
            a_step("TP", a)
            step("T1", c1)
            if end:
                a_step("CT", b + 1)
            if not end:
                step("PM", c2)
            step("N2", c0)
            if end:
                a_step("CB", b + 1)
            step("F", c1)
            step("N2", c1)
            if end:
                a_step("scale_b", b + 1)
                a_step("scale_a", b + 2)
                a_step("E0", b + 1)

        with eng.Fori(0, 3) as g:
            a = a_pair(g + 4) or [None, None]
            cs = quad(eng, b * 4 + g, g * 4)
            after = quad(eng, b * 4 + g + 1, g * 4 + 4)
            c_unit(a[0], cs[0], cs[1], cs[2], False)
            c_unit(a[1], cs[2], cs[3], after[0], False)
        a = a_pair(7) or [None, None]
        cs = quad(eng, b * 4 + 3, 12)
        c_unit(a[0], cs[0], cs[1], cs[2], False)
        c_unit(a[1], cs[2], cs[3], None, True)

    with eng.Fori(0, BATCHES - 1) as b:
        period(b, False)
    period(BATCHES - 1, True)


def build(nc, x, Wq, Wk, Wv, Wo, bo, kernel, bias, lora_a, lora_b, out):
    fp32, fp16, i32 = mybir.dt.float32, mybir.dt.float16, mybir.dt.int32
    ALU, ACT, AX = mybir.AluOpType, mybir.ActivationFunctionType, mybir.AxisListType
    ds = bass.ds

    x_rows = x.rearrange("b n d -> (b n) d")
    out_rows = out.rearrange("b n d -> (b n) d")

    ctx = ExitStack()
    with ctx:
        def sb(name, shape, dt):
            return ctx.enter_context(nc.sbuf_tensor(name, shape, dt))

        def sem(name):
            return ctx.enter_context(nc.semaphore(name))

        wq = sb("wq", [P, 2, CH, D], fp16)
        wk = sb("wk", [P, 2, CH, D], fp16)
        wvo = sb("wvo", [P, 2, CH, D], fp16)
        ffn = sb("ffn", [P, 2, CH, D], fp16)
        attn = sb("attn", [P, 2, CH, D], fp16)
        gt = sb("gt", [P, 2, CH, D], fp16)
        probs = sb("probs", [P, RING * 2 * D], fp16)
        keys = sb("keys", [P, TILES * D], fp32)
        xn = sb("xn", [P, TILES * 2 * D], fp16)
        x_in = [sb(f"x_in{i}", [P, D], fp32) for i in range(2)]
        x_abs = [sb(f"x_abs{i}", [P, D], fp32) for i in range(2)]
        xT = sb("xT", [P, 2, D], fp16)
        exp_q = sb("exp_q", [P, D], fp32)
        exp_k = [sb(f"exp_k{i}", [P, D], fp32) for i in range(2)]
        ek = [sb(f"ek{i}", [P, 2, D], fp16) for i in range(2)]
        kmax = sb("kmax", [P, D], fp32)
        ksum = sb("ksum", [P, D], fp32)
        kshift = sb("kshift", [P, D], fp32)
        bo_all = sb("bo_all", [P, D], fp32)
        bo_scaled = sb("bo_scaled", [P, D], fp32)
        bias_all = sb("bias_all", [P, D], fp32)
        y = [sb(f"y{i}", [P, D], fp32) for i in range(4)]
        x1T = sb("x1T", [P, 2, D], fp16)
        z = [sb(f"z{i}", [P, D], fp32) for i in range(2)]
        ident = sb("ident", [P, P], fp32)
        ones = sb("ones", [P, P], fp32)
        zeros = sb("zeros", [P, P], fp16)
        q_recip_all = sb("q_recip_all", [P, BATCHES * TILES], fp32)
        absmax_cols = sb("absmax_cols", [P, TILES], fp32)
        stats = sb("stats", [P, 4, 8], fp32)
        work = probs[:, :].bitcast(fp32)
        w32 = [work[:, i * CH * D:(i + 1) * CH * D].rearrange("p (c n) -> p c n", c=CH) for i in range(5)]

        def column(name, k=1):
            return sb(name, [P, k], fp32)[:, :]

        sx, isx, ax = column("sx"), column("isx"), column("ax")
        kq, kk = column("kq"), column("kk")
        s_attn, f_attn, g_attn = column("s_attn"), column("f_attn"), column("g_attn")
        k_ffn = column("k_ffn")
        sw, isw = column("sw", 4), column("isw", 4)
        b_attn, bo_max = column("b_attn"), column("bo_max")
        w_abs, w_abs_all = column("w_abs", 4), column("w_abs_all", 4)
        absmax_p, absmax_new = column("absmax_p"), column("absmax_new")
        q_sum, q_rowmax_c, q_bias_c = column("q_sum"), column("q_rowmax_c"), column("q_bias_c")
        rk, rkf, kmax_c = column("rk", CH), column("rkf", CH), column("kmax_c", CH)
        half_neg = column("half_neg")
        t0, t1, t2, t3 = (column(f"t{i}") for i in range(4))
        rqg, rstd1, rstd2 = ([column(f"{n}{i}") for i in range(2)] for n in ("rqg", "rstd1_", "rstd2_"))

        banks = [ctx.enter_context(nc.psum_tensor(f"bank{i}", [P, D], fp32)) for i in range(8)]
        TRANS, KEYS, QUERIES, MISC = banks[4:8]
        P_TRANS = MISC
        X1T_BANK, FFN_BANK = banks[2], banks[3]

        names = """x_scaled xT_psum xTh xTl k_psum q_psum k_stored k_max q_rowmax q_bias q_exp q_recip
            pT_psum pTh pTl xnh xn_split x_absmax k_shifted k_exp ekh ek_split k_summed g_psum
            rq_scaled attn_psum y_sum y_stats ln1_stats ln1_var ln1_rstd x1_ready x1T_psum x1Th x1T_split
            ffn_psum z_sum z_stats ln2_stats ln2_var ln2_rstd out_ready""".split()
        S = {name: sem(name) for name in names}
        x_in_loaded = [sem(f"x_in_loaded{i}") for i in range(2)]
        x_abs_loaded = [sem(f"x_abs_loaded{i}") for i in range(2)]
        y_loaded = [sem(f"y_loaded{i}") for i in range(4)]
        out_stored = [sem(f"out_stored{i}") for i in range(2)]
        kmaxT, kmax_col, kmax_reset, kmax_diag, kmax_row, kshift_ready = (sem(n) for n in (
            "kmaxT", "kmax_col", "kmax_reset", "kmax_diag", "kmax_row", "kshift_ready"))
        ksum_psum, ksum_recip, ksum_ready, ksum_reset = (sem(n) for n in (
            "ksum_psum", "ksum_recip", "ksum_ready", "ksum_reset"))
        gh, g_split, m_psum, m_sum, mh, m_split = (sem(n) for n in (
            "gh", "g_split", "m_psum", "m_sum", "mh", "m_split"))
        absmax_part, absmax_all, scale_a, scale_b = (sem(n) for n in (
            "absmax_part", "absmax_all", "scale_a", "scale_b"))
        rot_a, rot_b = sem("rot_a"), sem("rot_b")
        w_loaded = [sem(f"w_loaded{i}") for i in range(9)]
        pool_set, dve_set, act_set, pe_set, leads = (sem(n) for n in ("pool_set", "dve_set", "act_set", "pe_set", "leads"))
        setup_done, waited = sem("setup_done"), sem("waited")

        def apart(eng):
            eng.sem_inc(waited, 1)

        block = ctx.enter_context(nc.Block())

        @block.sync
        def _(sp):
            def setup():
                for k, (dst, w) in enumerate(((0, Wq), (1, Wk), (2, kernel), (3, Wv), (4, Wo))):
                    sp.dma_start(w32[dst], w.rearrange("(c p) n -> p c n", p=P)).then_inc(w_loaded[k], 16)
                sp.dma_start(x_in[0][:, 0:CH * RANK].rearrange("p (c r) -> p c r", c=CH),
                             lora_a.rearrange("(c p) r -> p c r", p=P)).then_inc(w_loaded[5], 16)
                sp.dma_start(x_in[1][0:RANK, :], lora_b).then_inc(w_loaded[6], 16)
                sp.dma_start(y[0][0:1, :], bo.rearrange("(a n) -> a n", a=1)).then_inc(w_loaded[7], 16)
                sp.dma_start(y[1][0:1, :], bias.rearrange("(a n) -> a n", a=1)).then_inc(w_loaded[8], 16)
                sp.wait_ge(setup_done, 1)
                sp.dma_start(x_in[0][:, :], x_rows[0:P, :]).then_inc(x_in_loaded[0], 16)
                for q in range(2):
                    sp.dma_start(y[q][:, :], x_rows[q * P:(q + 1) * P, :]).then_inc(y_loaded[q], 16)

            def X(x):
                sp.wait_ge(S["x_absmax"], done(x.n - 2))
                row = snapped(sp, x.n % (BATCHES * TILES) * P)
                sp.dma_start(x_abs[x.par][:, :], x_rows[ds(row, P), :]).then_inc(x_abs_loaded[x.par], 16)

            def Sx(a):
                sp.wait_ge(S["xn_split"], done(a.n - 1))
                sp.wait_ge(S["xT_psum"], done(a.n - 1))
                row = snapped(sp, (a.n + 1) % (BATCHES * TILES) * P)
                sp.dma_start(x_in[1 - a.par][:, :], x_rows[ds(row, P), :]).then_inc(x_in_loaded[1 - a.par], 16)

            def PM(c):
                if isinstance(c.n, int) and c.n + 2 >= BATCHES * TILES:
                    return
                sp.wait_ge(S["x1T_psum"], done(c.n - 2))
                row = snapped(sp, (c.n + 2) * P)
                q = (c.q + 2) % 4
                sp.dma_start(y[q][:, :], x_rows[ds(row, P), :]).then_inc(y_loaded[q], 16)

            def N2(c):
                sp.wait_ge(S["out_ready"], done(c.n))
                row = snapped(sp, c.n * P)
                sp.dma_start(out_rows[ds(row, P), :], z[c.par][:, :]).then_inc(out_stored[c.par], 16)

            walk(sp, {"setup": setup, "X": X, "Sx": Sx, "PM": PM, "N2": N2})
            for k in range(2):
                sp.wait_ge(out_stored[k], 16 * (BATCHES * TILES // 2 + 1))

        @block.gpsimd
        def _(pool):
            def setup():
                nc.gpsimd.memset(ident[:, :], 0.0).then_inc(pool_set, 1)
                nc.gpsimd.memset(ones[:, :], 1.0).then_inc(pool_set, 1)
                nc.gpsimd.memset(zeros[:, :], 0.0).then_inc(pool_set, 1)
                nc.gpsimd.memset(half_neg, -0.5).then_inc(pool_set, 1)
                nc.gpsimd.memset(ksum[:, :], 0.0).then_inc(pool_set, 1)
                pool.wait_ge(pool_set, 5)
                nc.gpsimd.affine_select(out=ident[:, :], in_=ident[:, :], compare_op=ALU.not_equal, fill=1.0,
                                        base=0, pattern=[[-1, P]], channel_multiplier=1).then_inc(pool_set, 1)
                pool.wait_ge(dve_set, 3)
                nc.gpsimd.partition_all_reduce(w_abs_all[:, 0:3], w_abs[:, 0:3], P, bass.bass_isa.ReduceOp.absmax
                                               ).then_inc(pool_set, 1)
                pool.wait_ge(absmax_part, 1)
                nc.gpsimd.partition_all_reduce(w_abs_all[:, 2:4], w_abs[:, 2:4], P, bass.bass_isa.ReduceOp.absmax
                                               ).then_inc(pool_set, 1)
                pool.wait_ge(setup_done, 1)

            def XS(s):
                pool.wait_ge(absmax_part, s + 2)
                pool.wait_ge(scale_a, s + 1)
                apart(pool)
                nc.gpsimd.partition_all_reduce(absmax_new, absmax_p, P, bass.bass_isa.ReduceOp.absmax
                                               ).then_inc(absmax_all, 1)

            def Lq(a):
                pool.wait_ge(S["xnh"], done(a.n))
                slot = snapped(pool, a.t * (2 * D))
                nc.gpsimd.tensor_tensor(xn[:, ds(slot + D, D)], x_in[a.par][:, :], xn[:, ds(slot, D)], ALU.subtract
                                        ).then_inc(S["xn_split"], 1)

            def shift(n, t, par):
                pool.wait_ge(S["ek_split"], done(n - 2))
                pool.wait_ge(S["k_summed"], done(n - 2))
                slot = snapped(pool, t * D)
                nc.gpsimd.tensor_tensor(exp_k[par][:, :], keys[:, ds(slot, D)], kshift[:, :], ALU.subtract
                                        ).then_inc(S["k_shifted"], 1)

            def CB(b):
                pool.wait_ge(kshift_ready, b + 1)
                shift(b * TILES, 0, 0)

            def E0(b):
                shift(b * TILES + 1, 1, 1)

            def B(k):
                pool.wait_ge(S["k_exp"], done(k.n))
                pool.wait_ge(S["k_summed"], done(k.n - 1))
                nc.gpsimd.tensor_tensor(ksum[:, :], ksum[:, :], exp_k[k.par][:, :], ALU.add
                                        ).then_inc(S["k_summed"], 1)
                if not (isinstance(k.t, int) and k.t >= TILES - 2):
                    shift(k.n + 2, k.t + 2, k.par)

            def KS(b):
                pool.wait_ge(ksum_psum, b + 1)
                apart(pool)
                nc.gpsimd.memset(ksum[:, :], 0.0).then_inc(ksum_reset, 1)

            def M(b, m):
                pool.wait_ge(mh, b * CH + m + 1)
                nc.gpsimd.tensor_tensor(attn[:, 1, m, :], exp_k[m % 2][:, :], attn[:, 0, m, :], ALU.subtract
                                        ).then_inc(m_split, 1)

            def PM(c):
                pool.wait_ge(S["q_recip"], done(c.n))
                pool.wait_ge(scale_b, c.quad // (TILES // 4) + 1)
                pool.wait_ge(S["y_sum"], done(c.n - 2))
                nc.gpsimd.tensor_tensor(rqg[c.par], q_recip_all[:, ds(c.n, 1)], g_attn, ALU.mult
                                        ).then_inc(S["rq_scaled"], 1)
                rstd(c, 2, rstd1, "ln1")

            def rstd(c, col, dst, ln):
                pool.wait_ge(S[ln + "_stats"], done(c.n))
                mv = stats[:, 2 * (col // 3) + c.par, 6:8]
                apart(pool)
                nc.gpsimd.tensor_scalar(mv[:, 1:2], mv[:, 1:2], EPS, 1.0, ALU.add, ALU.mult
                                        ).then_inc(S[ln + "_var"], 1)
                pool.wait_ge(S[ln + "_var"], done(c.n))
                nc.gpsimd.tensor_tensor(dst[c.par], mv[:, 1:2], half_neg, ALU.pow).then_inc(S[ln + "_rstd"], 1)

            def F(c):
                rstd(c, 3, rstd2, "ln2")

            walk(pool, {"setup": setup, "XS": XS, "Lq": Lq, "CB": CB, "E0": E0, "B": B, "KS": KS, "M": M,
                        "PM": PM, "F": F})

        @block.scalar
        def _(act):
            copy, identity, exp = ACT.Copy, ACT.Identity, ACT.Exp

            def setup():
                for m in range(CH):
                    act.wait_ge(pe_set, m + 1)
                    nc.scalar.activation(exp_wv(m), banks[m][:, :], copy).then_inc(act_set, 1)
                act.wait_ge(pe_set, 5)
                nc.scalar.activation(y[2][0:RANK, :], TRANS[0:RANK, :], copy).then_inc(act_set, 1)
                act.wait_ge(pe_set, 6)
                nc.scalar.activation(bo_all[:, :], KEYS[:, :], copy).then_inc(act_set, 1)
                act.wait_ge(pe_set, 7)
                nc.scalar.activation(bias_all[:, :], QUERIES[:, :], copy).then_inc(act_set, 1)
                for c in range(CH):
                    act.wait_ge(pe_set, 8 + c)
                    nc.scalar.activation(w32[3][:, c, :], banks[c][:, :], copy).then_inc(act_set, 1)
                act.wait_ge(setup_done, 1)

            def Sx(a):
                act.wait_ge(scale_a, a.n // TILES + 2)
                act.wait_ge(x_in_loaded[a.par], (a.half + 1) * 16)
                nc.scalar.activation(x_in[a.par][:, :], x_in[a.par][:, :], copy, scale=sx
                                     ).then_inc(S["x_scaled"], 1)

            def Tx(a):
                act.wait_ge(S["xT_psum"], done(a.n))
                act.wait_ge(S["k_psum"], done(a.n - 1))
                nc.scalar.activation(xT[:, 0, :], TRANS[:, :], copy).then_inc(S["xTh"], 1)
                act.wait_ge(S["x_scaled"], done(a.n))
                if not a.first:
                    act.wait_ge(S["g_psum"], done(a.n - TILES))
                slot = snapped(act, a.t * (2 * D))
                nc.scalar.activation(xn[:, ds(slot, D)], x_in[a.par][:, :], copy).then_inc(S["xnh"], 1)

            def Lk(a):
                act.wait_ge(S["k_psum"], done(a.n))
                if not a.first:
                    act.wait_ge(S["k_shifted"], done(a.n - TILES))
                slot = snapped(act, a.t * D)
                nc.scalar.activation(keys[:, ds(slot, D)], KEYS[:, :], copy).then_inc(S["k_stored"], 1)

            def Lq(a):
                act.wait_ge(S["q_bias"], done(a.n))
                act.wait_ge(S["pT_psum"], done(a.n - 1))
                act.wait_ge(S["q_recip"], done(a.n - 1))
                nc.scalar.activation(exp_q[:, :], QUERIES[:, :], exp, bias=q_bias_c, scale=kq,
                                     accum_out=q_sum).then_inc(S["q_exp"], 1)

            def TP(a):
                act.wait_ge(S["pT_psum"], done(a.n))
                slot = snapped(act, a.ring * (2 * D))
                nc.scalar.activation(probs[:, ds(slot, D)], P_TRANS[:, :], copy, scale=PS).then_inc(S["pTh"], 1)

            def CB(b):
                act.wait_ge(kmax_row, b + 1)
                nc.scalar.activation(kshift[:, :], MISC[:, :], copy).then_inc(kshift_ready, 1)

            def exponentials(n, par):
                act.wait_ge(S["k_shifted"], done(n))
                nc.scalar.activation(exp_k[par][:, :], exp_k[par][:, :], exp, scale=kk).then_inc(S["k_exp"], 1)

            def E0(b):
                act.wait_ge(scale_b, b + 1)
                exponentials(b * TILES, 0)

            def B(k):
                if not (isinstance(k.t, int) and k.t == TILES - 1):
                    exponentials(k.n + 1, 1 - k.par)

            def GE(b):
                act.wait_ge(S["g_psum"], done(b * TILES + TILES - 1))
                for c in range(CH):
                    nc.scalar.activation(gt[:, 0, c, :], banks[c][:, :], copy, scale=GS).then_inc(gh, 1)

            def M(b, m):
                act.wait_ge(m_sum, b * CH + m + 1)
                nc.scalar.activation(attn[:, 0, m, :], exp_k[m % 2][:, :], copy).then_inc(mh, 1)

            def T1(c):
                act.wait_ge(S["x1T_psum"], done(c.n))
                act.wait_ge(S["ffn_psum"], done(c.n - 1))
                nc.scalar.activation(x1T[:, 0, :], X1T_BANK[:, :], copy, scale=NS).then_inc(S["x1Th"], 1)

            def exp_wv(m):
                return keys[:, m * D:(m + 1) * D]

            walk(act, {"setup": setup, "Sx": Sx, "Tx": Tx, "Lk": Lk, "Lq": Lq, "TP": TP, "CB": CB, "E0": E0,
                       "B": B, "GE": GE, "M": M, "T1": T1})

        @block.vector
        def _(dve):
            V = nc.vector

            def power(dst, src, tmp, link):
                link(V.tensor_scalar(tmp, src, 1e-12, 1.0 / TOP, ALU.max, ALU.mult))
                link(V.reciprocal(tmp, tmp))
                link(V.tensor_scalar(dst.bitcast(i32), tmp.bitcast(i32), 0x7F800000, None, ALU.bitwise_and))

            def setup():
                chain = [0]

                def link(ins):
                    chain[0] += 1
                    ins.then_inc(dve_set, 1)
                    dve.wait_ge(dve_set, chain[0])

                for k in range(3):
                    dve.wait_ge(w_loaded[k], 16)
                    link(V.tensor_reduce(w_abs[:, k:k + 1], w32[k], AX.XY, ALU.max, apply_absolute_value=True))
                link(V.memset(kmax[:, :], FAR))
                dve.wait_ge(pool_set, 7)
                for k, w in ((0, wq), (1, wk)):
                    power(sw[:, k:k + 1], w_abs_all[:, k:k + 1], t0, link)
                    link(V.reciprocal(isw[:, k:k + 1], sw[:, k:k + 1]))
                    link(V.tensor_scalar(w[:, 0], w32[k], sw[:, k:k + 1], None, ALU.mult))
                    link(V.scalar_tensor_tensor(w[:, 1], w32[k], sw[:, k:k + 1], w[:, 0], ALU.mult, ALU.subtract))
                link(V.tensor_scalar(t1, w_abs_all[:, 2:3], 1.0 / 7.0, None, ALU.mult))
                link(V.reciprocal(t2, t1))
                big = 1.5 * 2.0 ** 23
                link(V.tensor_scalar(w32[2], w32[2], t2, big, ALU.mult, ALU.add))
                link(V.tensor_scalar(w32[2], w32[2], big, None, ALU.subtract))
                link(V.tensor_scalar(w32[2], w32[2], -8.0, 7.0, ALU.max, ALU.min))
                dve.wait_ge(pe_set, 15)
                for c in range(CH):
                    link(V.scalar_tensor_tensor(w32[2][:, c, :], w32[2][:, c, :], t1, banks[4 + c][:, :],
                                                ALU.mult, ALU.add))
                    diag = w32[2][:, c, c * P:(c + 1) * P]
                    link(V.tensor_tensor(diag, diag, ident[:, :], ALU.add))
                dve.wait_ge(act_set, 11)
                link(V.tensor_reduce(w_abs[:, 3:4], w32[3], AX.XY, ALU.max, apply_absolute_value=True))
                link(V.tensor_reduce(bo_max, bo_all[:, :], AX.X, ALU.max, apply_absolute_value=True))
                V.tensor_reduce(w_abs[:, 2:3], w32[2], AX.XY, ALU.max, apply_absolute_value=True).then_inc(absmax_part, 1)
                dve.wait_ge(pool_set, 8)
                for k, src, w in ((3, 2, ffn), (2, 3, wvo)):
                    power(sw[:, k:k + 1], w_abs_all[:, src:src + 1], t0, link)
                    link(V.reciprocal(isw[:, k:k + 1], sw[:, k:k + 1]))
                    link(V.tensor_scalar(w[:, 0], w32[src], sw[:, k:k + 1], None, ALU.mult))
                    link(V.scalar_tensor_tensor(w[:, 1], w32[src], sw[:, k:k + 1], w[:, 0], ALU.mult, ALU.subtract))
                link(V.tensor_scalar(b_attn, w_abs_all[:, 3:4], D * ATTN_SCALE, None, ALU.mult))
                link(V.tensor_scalar(k_ffn, isw[:, 3:4], 1.0 / NS, None, ALU.mult))
                link(V.memset(absmax_p, 0.0))
                for name in names:
                    dve.sem_inc(S[name], LEAD)
                for k in range(2):
                    dve.sem_inc(out_stored[k], 16)
                dve.sem_inc(scale_a, 1)
                dve.drain().then_inc(setup_done, 1)

            def X(x):
                dve.wait_ge(x_abs_loaded[x.par], (x.half + 1) * 16)
                V.tensor_reduce(absmax_cols[:, ds(x.t, 1)], x_abs[x.par][:, :], AX.X, ALU.max,
                                apply_absolute_value=True).then_inc(S["x_absmax"], 1)

            def XS(s):
                dve.wait_ge(S["x_absmax"], done(s * TILES + TILES - 1))
                dve.wait_ge(absmax_all, s) if not (isinstance(s, int) and s == 0) else None
                V.tensor_reduce(absmax_p, absmax_cols[:, :], AX.X, ALU.max).then_inc(absmax_part, 1)

            def linker(sem_, start):
                at = [start]

                def link(ins):
                    at[0] = at[0] + 1
                    ins.then_inc(sem_, 1)
                    dve.wait_ge(sem_, at[0])
                return link

            def scale_a_(s):
                dve.wait_ge(absmax_all, s + 1)
                dve.wait_ge(S["x_scaled"], done(s * TILES - 1))
                dve.wait_ge(S["q_exp"], done(s * TILES - 1))
                link = linker(rot_a, s * ROT_A_STEPS)
                link(V.tensor_scalar(ax, absmax_new, 1.0, None, ALU.mult))
                power(sx, ax, t3, link)
                link(V.reciprocal(isx, sx))
                V.tensor_scalar(kq, isx, isw[:, 0:1], None, ALU.mult).then_inc(scale_a, 1)

            def scale_b_(b):
                dve.wait_ge(S["k_exp"], done(b * TILES - 1))
                dve.wait_ge(S["rq_scaled"], done(b * TILES - 1))
                link = linker(rot_b, b * ROT_STEPS)
                link(V.tensor_scalar(kk, isx, isw[:, 1:2], None, ALU.mult))
                link(V.tensor_scalar(t0, ax, b_attn, bo_max, ALU.mult, ALU.add))
                power(s_attn, t0, t1, link)
                link(V.tensor_scalar(t0, s_attn, PS, None, ALU.mult))
                link(V.reciprocal(g_attn, t0))
                link(V.tensor_scalar(t0, isx, isw[:, 2:3], ATTN_SCALE / (GS * PS), ALU.mult, ALU.mult))
                link(V.tensor_scalar(f_attn, t0, s_attn, None, ALU.mult))
                V.tensor_scalar(bo_scaled[:, :], bo_all[:, :], s_attn, None, ALU.mult).then_inc(scale_b, 1)

            def Tx(a):
                dve.wait_ge(S["xTh"], done(a.n))
                V.tensor_tensor(xT[:, 1, :], TRANS[:, :], xT[:, 0, :], ALU.subtract).then_inc(S["xTl"], 1)

            def Lk(a):
                dve.wait_ge(S["k_stored"], done(a.n))
                dve.wait_ge(S["k_max"], done(a.n - 1))
                if not a.first:
                    dve.wait_ge(kmax_reset, a.n // TILES)
                slot = snapped(dve, a.t * D)
                V.tensor_tensor(kmax[:, :], kmax[:, :], keys[:, ds(slot, D)], ALU.max).then_inc(S["k_max"], 1)

            def Lq(a):
                dve.wait_ge(S["q_psum"], done(a.n))
                V.tensor_reduce(q_rowmax_c, QUERIES[:, :], AX.X, ALU.max, negate=True).then_inc(S["q_rowmax"], 1)
                dve.wait_ge(S["q_rowmax"], done(a.n))
                dve.wait_ge(S["q_exp"], done(a.n - 1))
                V.tensor_scalar(q_bias_c, q_rowmax_c, kq, None, ALU.mult).then_inc(S["q_bias"], 1)

            def TP(a):
                dve.wait_ge(S["q_exp"], done(a.n))
                V.reciprocal(q_recip_all[:, ds(a.n, 1)], q_sum).then_inc(S["q_recip"], 1)
                dve.wait_ge(S["pTh"], done(a.n))
                slot = snapped(dve, a.ring * (2 * D))
                V.scalar_tensor_tensor(probs[:, ds(slot + D, D)], P_TRANS[:, :], PS, probs[:, ds(slot, D)],
                                       ALU.mult, ALU.subtract).then_inc(S["pTl"], 1)

            def CT(b):
                dve.wait_ge(kmaxT, b + 1)
                V.memset(kmax[:, :], FAR).then_inc(kmax_reset, 1)
                V.tensor_reduce(kmax_c, MISC[:, :].rearrange("p (c n) -> p c n", c=CH), AX.X, ALU.max
                                ).then_inc(kmax_col, 1)
                dve.wait_ge(kmax_col, b + 1)
                V.tensor_tensor(exp_k[1][:, :].rearrange("p (c n) -> p c n", c=CH),
                                ident[:, :].unsqueeze(1).to_broadcast([P, CH, P]),
                                kmax_c.unsqueeze(2).to_broadcast([P, CH, P]), ALU.mult).then_inc(kmax_diag, 1)

            def split_e(n, par):
                dve.wait_ge(S["k_exp"], done(n))
                dve.wait_ge(S["g_psum"], done(n - 2))
                V.tensor_scalar(ek[par][:, 0, :], exp_k[par][:, :], PS, None, ALU.mult).then_inc(S["ekh"], 1)
                dve.wait_ge(S["ekh"], done(n))
                V.scalar_tensor_tensor(ek[par][:, 1, :], exp_k[par][:, :], PS, ek[par][:, 0, :],
                                       ALU.mult, ALU.subtract).then_inc(S["ek_split"], 1)

            def E0(b):
                split_e(b * TILES, 0)

            def B(k):
                if not (isinstance(k.t, int) and k.t == TILES - 1):
                    split_e(k.n + 1, 1 - k.par)

            def KS(b):
                dve.wait_ge(ksum_psum, b + 1)
                V.reciprocal(rk, MISC[:, 0:CH]).then_inc(ksum_recip, 1)
                dve.wait_ge(ksum_recip, b + 1)
                V.tensor_scalar(rkf, rk, f_attn, None, ALU.mult).then_inc(ksum_ready, 1)

            def GE(b):
                for c in range(CH):
                    dve.wait_ge(gh, b * CH + c + 1)
                    V.scalar_tensor_tensor(gt[:, 1, c, :], banks[c][:, :], GS, gt[:, 0, c, :],
                                           ALU.mult, ALU.subtract).then_inc(g_split, 1)

            def M(b, m):
                dve.wait_ge(m_psum, b * CH + m + 1)
                dve.wait_ge(ksum_ready, b + 1)
                if m < 2:
                    dve.wait_ge(S["k_summed"], done(b * TILES + TILES - 1))
                else:
                    dve.wait_ge(m_split, b * CH + m - 1)
                V.scalar_tensor_tensor(exp_k[m % 2][:, :], banks[m][:, :], rkf[:, m:m + 1], bo_scaled[:, :],
                                       ALU.mult, ALU.add).then_inc(m_sum, 1)

            def statistics(c, v, which, ln):
                V.bn_stats(stats[:, 2 * which + c.par, 0:6], v).then_inc(S["yz"[which] + "_stats"], 1)
                dve.wait_ge(S["yz"[which] + "_stats"], done(c.n))
                apart(dve)
                V.bn_aggr(stats[:, 2 * which + c.par, 6:8], stats[:, 2 * which + c.par, 0:6]
                          ).then_inc(S[ln + "_stats"], 1)

            def PM(c):
                dve.wait_ge(S["attn_psum"], done(c.n))
                dve.wait_ge(S["rq_scaled"], done(c.n))
                dve.wait_ge(y_loaded[c.q], (c.quad + 1) * 16)
                V.scalar_tensor_tensor(y[c.q][:, :], banks[c.par][:, :], rqg[c.par], y[c.q][:, :],
                                       ALU.mult, ALU.add).then_inc(S["y_sum"], 1)
                dve.wait_ge(S["y_sum"], done(c.n))
                statistics(c, y[c.q][:, :], 0, "ln1")

            def N1(c):
                dve.wait_ge(S["ln1_rstd"], done(c.n))
                V.tensor_scalar(y[c.q][:, :], y[c.q][:, :], stats[:, c.par, 6:7], rstd1[c.par],
                                ALU.subtract, ALU.mult).then_inc(S["x1_ready"], 1)

            def T1(c):
                dve.wait_ge(S["x1Th"], done(c.n))
                V.scalar_tensor_tensor(x1T[:, 1, :], X1T_BANK[:, :], NS, x1T[:, 0, :],
                                       ALU.mult, ALU.subtract).then_inc(S["x1T_split"], 1)

            def F(c):
                dve.wait_ge(S["ffn_psum"], done(c.n))
                dve.wait_ge(out_stored[c.par], (c.half + 1) * 16)
                V.scalar_tensor_tensor(z[c.par][:, :], FFN_BANK[:, :], k_ffn, bias_all[:, :],
                                       ALU.mult, ALU.add).then_inc(S["z_sum"], 1)
                dve.wait_ge(S["z_sum"], done(c.n))
                statistics(c, z[c.par][:, :], 1, "ln2")

            def N2(c):
                dve.wait_ge(S["ln2_rstd"], done(c.n))
                V.tensor_scalar(z[c.par][:, :], z[c.par][:, :], stats[:, 2 + c.par, 6:7], rstd2[c.par],
                                ALU.subtract, ALU.mult).then_inc(S["out_ready"], 1)

            walk(dve, {"setup": setup, "X": X, "XS": XS, "scale_a": scale_a_, "scale_b": scale_b_, "Tx": Tx,
                       "Lk": Lk, "Lq": Lq, "TP": TP, "CT": CT, "E0": E0, "B": B, "KS": KS, "GE": GE, "M": M, "PM": PM,
                       "N1": N1, "T1": T1, "F": F, "N2": N2})

        @block.tensor
        def _(pe):
            mm = nc.tensor.matmul

            def chunk(c):
                return slice(c * P, (c + 1) * P)

            def transposes(bank, src):
                for c in range(CH):
                    last = nc.tensor.transpose(bank[:, chunk(c)], src[:, chunk(c)], ident[:, :])
                return last

            def split_product(bank, left, right, start=True, stop=True):
                for c in range(CH):
                    mm(bank, left(0, c), right(0, c), start=start and c == 0, stop=False)
                    mm(bank, left(0, c), right(1, c), start=False, stop=False)
                    last = mm(bank, left(1, c), right(0, c), start=False, stop=stop and c == CH - 1)
                return last

            def setup():
                pe.wait_ge(pool_set, 6)
                pe.wait_ge(w_loaded[3], 16)
                for m in range(CH):
                    for c in range(CH):
                        last = nc.tensor.transpose(banks[m][:, chunk(c)], w32[3][:, c, chunk(m)], ident[:, :])
                    last.then_inc(pe_set, 1)
                pe.wait_ge(w_loaded[5], 16)
                for c in range(CH):
                    last = nc.tensor.transpose(TRANS[0:RANK, chunk(c)], x_in[0][:, c * RANK:(c + 1) * RANK],
                                               ident[:, :])
                last.then_inc(pe_set, 1)
                pe.wait_ge(w_loaded[7], 16)
                mm(KEYS[:, :], ones[0:1, :], y[0][0:1, :], start=True, stop=True).then_inc(pe_set, 1)
                pe.wait_ge(w_loaded[8], 16)
                mm(QUERIES[:, :], ones[0:1, :], y[1][0:1, :], start=True, stop=True).then_inc(pe_set, 1)
                pe.wait_ge(w_loaded[4], 16)
                pe.wait_ge(act_set, 4)
                for c in range(CH):
                    for m in range(CH):
                        last = mm(banks[c][:, :], keys[:, m * D + c * P:m * D + (c + 1) * P], w32[4][:, m, :],
                                  start=m == 0, stop=m == CH - 1)
                    last.then_inc(pe_set, 1)
                pe.wait_ge(w_loaded[6], 16)
                pe.wait_ge(act_set, 7)
                for c in range(CH):
                    mm(banks[4 + c][:, :], y[2][0:RANK, chunk(c)], x_in[1][0:RANK, :], start=True, stop=True
                       ).then_inc(pe_set, 1)
                pe.wait_ge(setup_done, 1)

            def Tx(a):
                pe.wait_ge(S["x_scaled"], done(a.n))
                pe.wait_ge(S["xTl"], done(a.n - 1))
                transposes(TRANS, x_in[a.par]).then_inc(S["xT_psum"], 1)

            def from_xT(part, c):
                return xT[:, part, chunk(c)]

            def Lk(a):
                pe.wait_ge(S["k_stored"], done(a.n - 1))
                split_product(KEYS[:, :], from_xT, lambda part, c: wk[:, part, c, :]).then_inc(S["k_psum"], 1)

            def Lq(a):
                pe.wait_ge(S["xTl"], done(a.n))
                pe.wait_ge(S["q_exp"], done(a.n - 1))
                split_product(QUERIES[:, :], from_xT, lambda part, c: wq[:, part, c, :]).then_inc(S["q_psum"], 1)

            def TP(a):
                pe.wait_ge(S["q_exp"], done(a.n))
                pe.wait_ge(S["pTl"], done(a.n - 1))
                if isinstance(a.t, int) and a.t == 6:
                    pe.wait_ge(ksum_recip, a.n // TILES)
                transposes(P_TRANS, exp_q).then_inc(S["pT_psum"], 1)

            def CT(b):
                pe.wait_ge(S["k_max"], done(b * TILES + TILES - 1))
                pe.wait_ge(S["pTl"], done(b * TILES + TILES - 1))
                transposes(MISC, kmax).then_inc(kmaxT, 1)

            def CB(b):
                pe.wait_ge(kmax_diag, b + 1)
                mm(MISC[:, :], ones[:, :], exp_k[1][:, :], start=True, stop=True).then_inc(kmax_row, 1)

            def clear(b):
                pe.wait_ge(S["z_sum"], done(b * TILES - 1))
                pe.wait_ge(S["y_sum"], done(b * TILES - 1))
                for c in range(CH):
                    mm(banks[c][:, :], zeros[:, :], wq[:, 0, 0, :], start=True, stop=False)

            def B(k):
                pe.wait_ge(S["ek_split"], done(k.n))
                pe.wait_ge(S["xn_split"], done(k.n))
                slot = snapped(pe, k.t * (2 * D))
                end = isinstance(k.t, int) and k.t == TILES - 1
                for c in range(CH):
                    high = xn[:, ds(slot + c * P, P)]
                    low = xn[:, ds(slot + (D + c * P), P)]
                    mm(banks[c][:, :], high, ek[k.par][:, 0, :], start=False, stop=False)
                    mm(banks[c][:, :], high, ek[k.par][:, 1, :], start=False, stop=False)
                    last = mm(banks[c][:, :], low, ek[k.par][:, 0, :], start=False, stop=end)
                last.then_inc(S["g_psum"], 1)

            def KS(b):
                pe.wait_ge(S["k_summed"], done(b * TILES + TILES - 1))
                pe.wait_ge(S["pTl"], done(BATCHES * TILES - 1 if isinstance(b, int) else (b + 1) * TILES + 5))
                for c in range(CH):
                    last = mm(MISC[:, c:c + 1], ksum[:, chunk(c)], ones[:, 0:1], start=True, stop=True)
                last.then_inc(ksum_psum, 1)

            def M(b, m):
                pe.wait_ge(g_split, b * CH + CH)
                split_product(banks[m][:, :], lambda part, c: gt[:, part, c, chunk(m)],
                              lambda part, c: wvo[:, part, c, :]).then_inc(m_psum, 1)

            def PM(c):
                pe.wait_ge(m_split, (c.quad // (TILES // 4) + 1) * CH)
                pe.wait_ge(S["pTl"], done(c.n))
                pe.wait_ge(S["y_sum"], done(c.n - 2))
                slot = snapped(pe, c.ring * (2 * D))
                split_product(banks[c.par][:, :], lambda part, k: probs[:, ds(slot + (part * D + k * P), P)],
                              lambda part, k: attn[:, part, k, :]).then_inc(S["attn_psum"], 1)

            def T1(c):
                pe.wait_ge(S["x1_ready"], done(c.n))
                pe.wait_ge(S["x1T_split"], done(c.n - 1))
                transposes(X1T_BANK, y[c.q]).then_inc(S["x1T_psum"], 1)

            def F(c):
                pe.wait_ge(S["x1T_split"], done(c.n))
                pe.wait_ge(S["z_sum"], done(c.n - 1))
                split_product(FFN_BANK[:, :], lambda part, k: x1T[:, part, chunk(k)],
                              lambda part, k: ffn[:, part, k, :]).then_inc(S["ffn_psum"], 1)

            walk(pe, {"setup": setup, "Tx": Tx, "Lk": Lk, "Lq": Lq, "TP": TP, "CT": CT, "CB": CB, "B": B,
                      "scale_b": clear, "KS": KS, "M": M, "PM": PM, "T1": T1, "F": F})


_INS = {"x": "L0_attn_x", "Wq": "L0_attn_Wq", "Wk": "L0_attn_Wk", "Wv": "L0_attn_Wv", "Wo": "L0_attn_Wo",
        "bo": "L0_attn_bo", "kernel": "L0_ffn_kernel", "bias": "L0_ffn_bias", "lora_a": "L0_ffn_a",
        "lora_b": "L0_ffn_b"}


def kernel(**inputs):
    import numpy as np
    import concourse.bacc as bacc
    from concourse.bass_utils import run_bass_kernel_spmd

    nc = bacc.Bacc("TRN2", target_bir_lowering=False, num_devices=1, dynamic_dma_scratch_size=4096)
    arrays, args = {}, {}
    for arg, name in _INS.items():
        a = np.ascontiguousarray(inputs[name])
        arrays[f"in_{arg}"] = a
        args[arg] = nc.dram_tensor(f"in_{arg}", a.shape, mybir.dt.from_np(a.dtype), kind="ExternalInput").ap()
    shape = (BATCHES, TOKENS, D)
    args["out"] = nc.dram_tensor("out_dram", shape, mybir.dt.float32, kind="ExternalOutput").ap()
    build(nc, **args)
    r = run_bass_kernel_spmd(nc, [arrays], core_ids=[0])
    return r.results[0]["out_dram"]
```

```python
import concourse.bass as bass
from concourse import mybir
from contextlib import ExitStack


P = 128
BATCHES, TOKENS, D = 8, 2048, 512
RANK = 16
CH = D // P
TILES = TOKENS // P
RING = 24
LEAD = 4
EPS = 1e-5
ATTN_SCALE = 1.0 / (D // 16) ** 0.5 / D
FAR = -3.0e38
PS = 4096.0
NS = 512.0
GS = 2.0 ** -22
TOP = 2.0 ** 13
ROT_STEPS = 9
ROT_A_STEPS = 5


def done(n):
    return n + 1 + LEAD


class Tile:

    def __init__(self, n, t, half, quad, q, ring, first=False):
        self.first = first
        self.n, self.t, self.half, self.quad, self.q, self.ring = n, t, half, quad, q, ring
        self.par = q % 2


def snapped(eng, value):
    return value if isinstance(value, int) else eng.snap(value)


def pair(eng, p, t, first=False):
    p = snapped(eng, p)
    n, ring = snapped(eng, p * 2), snapped(eng, p % (RING // 2) * 2)
    return [Tile(n + k, t + k, p, None, k, ring + k, first) for k in range(2)]


def quad(eng, p, t, first=False):
    p = snapped(eng, p)
    n, ring = snapped(eng, p * 4), snapped(eng, p % (RING // 4) * 4)
    return [Tile(n + k, t + k, p * 2 + k // 2, p, k, ring + k, first) for k in range(4)]


def walk(eng, do):

    def step(name, *args):
        if name in do:
            do[name](*args)

    step("setup")
    with eng.Fori(0, TILES // 4) as g:
        for x in quad(eng, g, g * 4):
            step("X", x)
    step("XS", 0)
    step("scale_a", 0)

    def a_alone(a, following, x):
        if following is not None:
            step("Sx", following)
        step("Lq", a)
        if following is not None:
            step("Tx", following)
        step("Lk", a)
        step("X", x)
        step("TP", a)

    per = TILES // 4
    a, x = quad(eng, 0, 0, True), quad(eng, per, 0)
    a.append(quad(eng, 1, 4, True)[0])
    step("Sx", a[0])
    step("Tx", a[0])
    for k in range(4):
        a_alone(a[k], a[k + 1], x[k])
        step("weights", k)
    with eng.Fori(1, per - 1) as g:
        a, x = quad(eng, g, g * 4, True), quad(eng, g + per, g * 4)
        a.append(quad(eng, g + 1, g * 4 + 4, True)[0])
        for k in range(4):
            a_alone(a[k], a[k + 1], x[k])
    a, x = quad(eng, per - 1, TILES - 4, True), quad(eng, 2 * per - 1, TILES - 4)
    a.append(None)
    for k in range(4):
        a_alone(a[k], a[k + 1], x[k])
    step("XS", 1)
    step("CT", 0)
    step("scale_b", 0)
    step("CB", 0)
    step("E0", 0)
    step("scale_a", 1)
    a = pair(eng, TILES // 2, 0)
    step("Sx", a[0])
    step("Tx", a[0])
    step("clear", 0)

    def period(b, last):

        def a_tiles(i, odd=0):
            if last:
                return [None] * 3
            both = pair(eng, (b + 1) * (TILES // 2) + i, i * 2) + pair(eng, (b + 1) * (TILES // 2) + i + 1, i * 2 + 2)
            return both[odd:odd + 3]

        def a_step(name, a):
            if not last and a is not None:
                step(name, a)

        def b_unit(a, following, bs, xs):
            step("B", bs[0])
            a_step("Sx", following)
            a_step("Lq", a)
            a_step("Tx", following)
            a_step("X", xs[0])
            step("B", bs[1])
            a_step("Lk", a)
            a_step("X", xs[1])
            a_step("TP", a)

        def quads(i):
            return quad(eng, b * per + i, i * 4), [None] * 4 if last else quad(eng, (b + 2) * per + i, i * 4)

        with eng.Fori(0, 3) as g:
            a = a_tiles(g)
            bs, xs = quads(g)
            b_unit(a[0], a[1], bs[0:2], xs[0:2])
            b_unit(a[1], a[2], bs[2:4], xs[2:4])
        a = a_tiles(3)
        bs, xs = quads(3)
        b_unit(a[0], a[1], bs[0:2], xs[0:2])
        for k in range(2, 4):
            step("B", bs[k])
            a_step("X", xs[k])
        step("KS", b)
        step("GE", b)
        a_step("Sx", a[2])
        a_step("Lq", a[1])
        a_step("Tx", a[2])
        a_step("Lk", a[1])
        step("M", b, 0)
        a_step("TP", a[1])
        step("M", b, 1)
        step("M", b, 2)
        step("M", b, 3)
        a_step("XS", b + 2)
        a = a_tiles(4)
        a_step("Sx", a[1])
        a_step("Lq", a[0])
        a_step("Tx", a[1])
        a_step("Lk", a[0])
        cs = quad(eng, b * per, 0)
        step("PM", cs[0])
        a_step("TP", a[0])
        step("N1", cs[0])
        step("PM", cs[1])

        def c_unit(a, following, c, ahead, end=0):
            step("T1", c[0])
            if end == 1:
                a_step("CB", b + 1)
            a_step("Sx", following)
            a_step("Lq", a)
            step("N1", c[1])
            if end != 1:
                step("PM", ahead[0])
            step("F", c[0])
            a_step("Tx", following)
            step("T1", c[1])
            a_step("Lk", a)
            if end == 1:
                a_step("E0", b + 1)
            step("N2", c[0])
            if end != 1:
                step("N1", ahead[0])
                step("PM", ahead[1])
            a_step("TP", a)
            if end == 2:
                a_step("CT", b + 1)
            step("F", c[1])
            step("N2", c[1])
            if end == 2:
                a_step("scale_b", b + 1)

        with eng.Fori(0, 3) as g:
            a = a_tiles(g + 4, 1)
            cs = quad(eng, b * per + g, g * 4)
            ahead = quad(eng, b * per + g + 1, g * 4 + 4)
            c_unit(a[0], a[1], cs[0:2], cs[2:4])
            c_unit(a[1], a[2], cs[2:4], ahead[0:2])
        a = a_tiles(7, 1)
        cs = quad(eng, b * per + 3, 12)
        c_unit(a[0], None, cs[0:2], cs[2:4], end=2)
        c_unit(None, None, cs[2:4], None, end=1)
        if not last:
            step("scale_a", b + 2)
            a = pair(eng, (b + 2) * (TILES // 2), 0)
            step("Sx", a[0])
            step("Tx", a[0])
            step("clear", b + 1)

    with eng.Fori(0, BATCHES - 1) as b:
        period(b, False)
    period(BATCHES - 1, True)


def build(nc, x, Wq, Wk, Wv, Wo, bo, kernel, bias, lora_a, lora_b, out):
    fp32, fp16, i32 = mybir.dt.float32, mybir.dt.float16, mybir.dt.int32
    ALU, ACT, AX = mybir.AluOpType, mybir.ActivationFunctionType, mybir.AxisListType
    ds = bass.ds

    x_rows = x.rearrange("b n d -> (b n) d")
    out_rows = out.rearrange("b n d -> (b n) d")

    ctx = ExitStack()
    with ctx:
        def sb(name, shape, dt):
            return ctx.enter_context(nc.sbuf_tensor(name, shape, dt))

        def sem(name):
            return ctx.enter_context(nc.semaphore(name))

        wq = sb("wq", [P, 2, CH, D], fp16)
        wk = sb("wk", [P, 2, CH, D], fp16)
        wvo = sb("wvo", [P, 2, CH, D], fp16)
        ffn = sb("ffn", [P, 2, CH, D], fp16)
        attn = sb("attn", [P, 2, CH, D], fp16)
        gt = sb("gt", [P, 2, CH, D], fp16)
        probs = sb("probs", [P, RING * 2 * D], fp16)
        keys = sb("keys", [P, TILES * D], fp32)
        xn = sb("xn", [P, TILES * 2 * D], fp16)
        x_in = [sb(f"x_in{i}", [P, D], fp32) for i in range(2)]
        x_abs = [sb(f"x_abs{i}", [P, D], fp32) for i in range(4)]
        xT = [sb(f"xT{i}", [P, 2, D], fp16) for i in range(2)]
        exp_q = sb("exp_q", [P, D], fp32)
        exp_k = [sb(f"exp_k{i}", [P, D], fp32) for i in range(2)]
        ek = [sb(f"ek{i}", [P, 2, D], fp16) for i in range(2)]
        kmax = sb("kmax", [P, D], fp32)
        ksum = sb("ksum", [P, D], fp32)
        kshift = sb("kshift", [P, D], fp32)
        bo_all = sb("bo_all", [P, D], fp32)
        bo_scaled = sb("bo_scaled", [P, D], fp32)
        bias_all = sb("bias_all", [P, D], fp32)
        y = [sb(f"y{i}", [P, D], fp32) for i in range(4)]
        x1T = sb("x1T", [P, 2, D], fp16)
        z = [sb(f"z{i}", [P, D], fp32) for i in range(2)]
        ident = sb("ident", [P, P], fp32)
        ones = sb("ones", [P, P], fp32)
        zeros = sb("zeros", [P, P], fp16)
        q_recip_all = sb("q_recip_all", [P, BATCHES * TILES], fp32)
        absmax_cols = sb("absmax_cols", [P, TILES], fp32)
        stats = sb("stats", [P, 4, 8], fp32)
        def matrix(t):
            return t.rearrange("p (c n) -> p c n", c=CH)

        wq32, wk32 = matrix(keys[:, 0:CH * D]), matrix(keys[:, CH * D:2 * CH * D])
        late = probs[:, TILES * 2 * D:RING * 2 * D].bitcast(fp32)
        ffn32, wo32 = matrix(late[:, 0:CH * D]), matrix(late[:, CH * D:2 * CH * D])
        wv32 = gt[:, :, :, :].rearrange("p h c n -> p (h c n)").bitcast(fp32)
        wvo32 = wv32 = matrix(wv32)
        wvT = matrix(attn[:, :, :, :].rearrange("p h c n -> p (h c n)").bitcast(fp32))
        a32, aT, b32 = z[0][:, 0:CH * RANK], z[1][0:RANK, :], exp_k[0][0:RANK, :]
        bo_row, bias_row = exp_k[1][0:1, :], kshift[0:1, :]

        def column(name, k=1):
            return sb(name, [P, k], fp32)[:, :]

        sx, isx, ax = column("sx"), column("isx"), column("ax")
        kq, kk = column("kq"), column("kk")
        s_attn, f_attn, g_attn = column("s_attn"), column("f_attn"), column("g_attn")
        k_ffn = column("k_ffn")
        sw, isw = column("sw", 4), column("isw", 4)
        b_attn, bo_max = column("b_attn"), column("bo_max")
        w_abs, w_abs_all = column("w_abs", 5), column("w_abs_all", 5)
        absmax_p, absmax_new = column("absmax_p"), column("absmax_new")
        q_sum, q_rowmax_c, q_bias_c = column("q_sum"), column("q_rowmax_c"), column("q_bias_c")
        rk, rkf, kmax_c = column("rk", CH), column("rkf", CH), column("kmax_c", CH)
        half_neg = column("half_neg")
        t0, t1, t2, t3 = (column(f"t{i}") for i in range(4))
        rqg, rstd1, rstd2 = ([column(f"{n}{i}") for i in range(2)] for n in ("rqg", "rstd1_", "rstd2_"))

        banks = [ctx.enter_context(nc.psum_tensor(f"bank{i}", [P, D], fp32)) for i in range(8)]
        TRANS, KEYS, QUERIES, MISC = banks[4:8]
        P_TRANS = MISC
        X1T_BANK, FFN_BANK = banks[2], banks[3]

        names = """x_scaled xT_psum xTh xTl k_psum q_psum k_stored k_max q_rowmax q_bias q_exp q_recip
            pT_psum pTh pTl xnh xn_split x_absmax k_shifted k_exp ekh ek_split k_summed g_psum
            rq_scaled attn_psum y_sum y_stats ln1_stats ln1_var ln1_rstd x1_ready x1T_psum x1Th x1T_split
            ffn_psum z_sum z_stats ln2_stats ln2_var ln2_rstd out_ready""".split()
        S = {name: sem(name) for name in names}
        x_in_loaded = [sem(f"x_in_loaded{i}") for i in range(2)]
        x_abs_loaded = [sem(f"x_abs_loaded{i}") for i in range(4)]
        y_loaded = [sem(f"y_loaded{i}") for i in range(4)]
        out_stored = [sem(f"out_stored{i}") for i in range(2)]
        kmaxT, kmax_col, kmax_reset, kmax_diag, kmax_row, kshift_ready = (sem(n) for n in (
            "kmaxT", "kmax_col", "kmax_reset", "kmax_diag", "kmax_row", "kshift_ready"))
        ksum_psum, ksum_recip, ksum_ready, ksum_reset = (sem(n) for n in (
            "ksum_psum", "ksum_recip", "ksum_ready", "ksum_reset"))
        gh, g_split, m_psum, m_sum, mh, m_split = (sem(n) for n in (
            "gh", "g_split", "m_psum", "m_sum", "mh", "m_split"))
        absmax_part, absmax_all, scale_a, scale_b = (sem(n) for n in (
            "absmax_part", "absmax_all", "scale_a", "scale_b"))
        rot_a, rot_b = sem("rot_a"), sem("rot_b")
        wq_loaded, wk_loaded, wv_loaded, wo_loaded, ffn_loaded, a_loaded, b_loaded, bo_loaded, bias_loaded = (
            sem(n) for n in ("wq_loaded", "wk_loaded", "wv_loaded", "wo_loaded", "ffn_loaded", "a_loaded",
                             "b_loaded", "bo_loaded", "bias_loaded"))
        rows_psum, rows_all, wv_psum, wvT_ready, aT_psum, aT_ready, wvo_psum, wvo_ready, ab_psum = (
            sem(n) for n in ("rows_psum", "rows_all", "wv_psum", "wvT_ready", "aT_psum", "aT_ready", "wvo_psum",
                             "wvo_ready", "ab_psum"))
        consts, dve_set, w_absmax, w_absmax_all, wqk_split, weights_split = (
            sem(n) for n in ("consts", "dve_set", "w_absmax", "w_absmax_all", "wqk_split", "weights_split"))
        setup_done, waited = sem("setup_done"), sem("waited")

        def apart(eng):
            eng.sem_inc(waited, 1)

        block = ctx.enter_context(nc.Block())

        @block.sync
        def _(sp):
            def setup():
                for row, src, there in ((bo_row, bo, bo_loaded), (bias_row, bias, bias_loaded)):
                    sp.dma_start(row, src.rearrange("(a n) -> a n", a=1)).then_inc(there, 16)
                for dst, w, there in ((wq32, Wq, wq_loaded), (wk32, Wk, wk_loaded)):
                    sp.dma_start(dst, w.rearrange("(c p) n -> p c n", p=P)).then_inc(there, 16)
                sp.wait_ge(setup_done, 1)

            def scale_a_(s):
                if not (isinstance(s, int) and s == 0):
                    return
                for k in range(2):
                    sp.dma_start(x_in[k][:, :], x_rows[k * P:(k + 1) * P, :]).then_inc(x_in_loaded[k], 16)
                for dst, w, there in ((wv32, Wv, wv_loaded), (wo32, Wo, wo_loaded), (ffn32, kernel, ffn_loaded)):
                    sp.dma_start(dst, w.rearrange("(c p) n -> p c n", p=P)).then_inc(there, 16)
                sp.dma_start(a32.rearrange("p (c r) -> p c r", c=CH),
                             lora_a.rearrange("(c p) r -> p c r", p=P)).then_inc(a_loaded, 16)
                sp.dma_start(b32, lora_b).then_inc(b_loaded, 16)
                for q in range(4):
                    sp.dma_start(y[q][:, :], x_rows[q * P:(q + 1) * P, :]).then_inc(y_loaded[q], 16)

            def X(x):
                sp.wait_ge(S["x_absmax"], done(x.n - 4))
                row = snapped(sp, x.n % (BATCHES * TILES) * P)
                sp.dma_start(x_abs[x.q][:, :], x_rows[ds(row, P), :]).then_inc(x_abs_loaded[x.q], 16)

            def Lk(a):
                sp.wait_ge(S["xn_split"], done(a.n))
                sp.wait_ge(S["xT_psum"], done(a.n))
                row = snapped(sp, (a.n + 2) % (BATCHES * TILES) * P)
                sp.dma_start(x_in[a.par][:, :], x_rows[ds(row, P), :]).then_inc(x_in_loaded[a.par], 16)

            def T1(c):
                if isinstance(c.n, int) and c.n + 4 >= BATCHES * TILES:
                    return
                sp.wait_ge(S["x1T_psum"], done(c.n))
                row = snapped(sp, (c.n + 4) * P)
                sp.dma_start(y[c.q][:, :], x_rows[ds(row, P), :]).then_inc(y_loaded[c.q], 16)

            def N2(c):
                sp.wait_ge(S["out_ready"], done(c.n))
                row = snapped(sp, c.n * P)
                sp.dma_start(out_rows[ds(row, P), :], z[c.par][:, :]).then_inc(out_stored[c.par], 16)

            walk(sp, {"setup": setup, "scale_a": scale_a_, "X": X, "Lk": Lk, "T1": T1, "N2": N2})
            for k in range(2):
                sp.wait_ge(out_stored[k], 16 * (BATCHES * TILES // 2 + 1))

        @block.gpsimd
        def _(pool):
            def setup():
                nc.gpsimd.memset(ident[:, :], 0.0).then_inc(consts, 1)
                nc.gpsimd.memset(ones[:, :], 1.0).then_inc(consts, 1)
                nc.gpsimd.memset(zeros[:, :], 0.0).then_inc(consts, 1)
                nc.gpsimd.memset(half_neg, -0.5).then_inc(consts, 1)
                nc.gpsimd.memset(ksum[:, :], 0.0).then_inc(consts, 1)
                pool.wait_ge(consts, 5)
                nc.gpsimd.affine_select(out=ident[:, :], in_=ident[:, :], compare_op=ALU.not_equal, fill=1.0,
                                        base=0, pattern=[[-1, P]], channel_multiplier=1).then_inc(consts, 1)
                largest(0, 0, 2)
                pool.wait_ge(setup_done, 1)

            def largest(k, lo, hi):
                pool.wait_ge(w_absmax, k + 1)
                nc.gpsimd.partition_all_reduce(w_abs_all[:, lo:hi], w_abs[:, lo:hi], P,
                                               bass.bass_isa.ReduceOp.absmax).then_inc(w_absmax_all, 1)

            def weights(k):
                if k == 0:
                    largest(1, 4, 5)
                if k == 2:
                    largest(2, 2, 4)

            def XS(s):
                pool.wait_ge(absmax_part, s + 2)
                pool.wait_ge(scale_a, s + 1)
                apart(pool)
                nc.gpsimd.partition_all_reduce(absmax_new, absmax_p, P, bass.bass_isa.ReduceOp.absmax
                                               ).then_inc(absmax_all, 1)

            def Lk(a):
                pool.wait_ge(S["xnh"], done(a.n))
                slot = snapped(pool, a.t * (2 * D))
                nc.gpsimd.tensor_tensor(xn[:, ds(slot + D, D)], x_in[a.par][:, :], xn[:, ds(slot, D)], ALU.subtract
                                        ).then_inc(S["xn_split"], 1)

            def shift(n, t, par):
                pool.wait_ge(S["ek_split"], done(n - 2))
                pool.wait_ge(S["k_summed"], done(n - 2))
                slot = snapped(pool, t * D)
                nc.gpsimd.tensor_tensor(exp_k[par][:, :], keys[:, ds(slot, D)], kshift[:, :], ALU.subtract
                                        ).then_inc(S["k_shifted"], 1)

            def CB(b):
                pool.wait_ge(kshift_ready, b + 1)
                shift(b * TILES, 0, 0)

            def E0(b):
                shift(b * TILES + 1, 1, 1)

            def B(k):
                pool.wait_ge(S["k_exp"], done(k.n))
                pool.wait_ge(S["k_summed"], done(k.n - 1))
                nc.gpsimd.tensor_tensor(ksum[:, :], ksum[:, :], exp_k[k.par][:, :], ALU.add
                                        ).then_inc(S["k_summed"], 1)
                if not (isinstance(k.t, int) and k.t >= TILES - 2):
                    shift(k.n + 2, k.t + 2, k.par)

            def KS(b):
                pool.wait_ge(ksum_psum, b + 1)
                apart(pool)
                nc.gpsimd.memset(ksum[:, :], 0.0).then_inc(ksum_reset, 1)

            def M(b, m):
                pool.wait_ge(mh, b * CH + m + 1)
                nc.gpsimd.tensor_tensor(attn[:, 1, m, :], exp_k[m % 2][:, :], attn[:, 0, m, :], ALU.subtract
                                        ).then_inc(m_split, 1)

            def PM(c):
                pool.wait_ge(S["q_recip"], done(c.n))
                pool.wait_ge(scale_b, c.quad // (TILES // 4) + 1)
                pool.wait_ge(S["y_sum"], done(c.n - 2))
                nc.gpsimd.tensor_tensor(rqg[c.par], q_recip_all[:, ds(c.n, 1)], g_attn, ALU.mult
                                        ).then_inc(S["rq_scaled"], 1)
                rstd(c, 2, rstd1, "ln1")

            def rstd(c, col, dst, ln):
                pool.wait_ge(S[ln + "_stats"], done(c.n))
                mv = stats[:, 2 * (col // 3) + c.par, 6:8]
                apart(pool)
                nc.gpsimd.tensor_scalar(mv[:, 1:2], mv[:, 1:2], EPS, 1.0, ALU.add, ALU.mult
                                        ).then_inc(S[ln + "_var"], 1)
                pool.wait_ge(S[ln + "_var"], done(c.n))
                nc.gpsimd.tensor_tensor(dst[c.par], mv[:, 1:2], half_neg, ALU.pow).then_inc(S[ln + "_rstd"], 1)

            def F(c):
                rstd(c, 3, rstd2, "ln2")

            walk(pool, {"setup": setup, "weights": weights, "XS": XS, "Lk": Lk, "CB": CB, "E0": E0, "B": B, "KS": KS, "M": M,
                        "PM": PM, "F": F})

        @block.scalar
        def _(act):
            copy, identity, exp = ACT.Copy, ACT.Identity, ACT.Exp

            def setup():
                for k, (dst, bank) in enumerate(((bo_all, KEYS), (bias_all, QUERIES))):
                    act.wait_ge(rows_psum, k + 1)
                    nc.scalar.activation(dst[:, :], bank[:, :], copy).then_inc(rows_all, 1)
                act.wait_ge(setup_done, 1)

            def weights(k):
                if k == 0:
                    for m in range(CH):
                        act.wait_ge(wv_psum, m + 1)
                        nc.scalar.activation(wvT[:, m, :], banks[m][:, :], copy).then_inc(wvT_ready, 1)
                if k == 1:
                    for c in range(CH):
                        act.wait_ge(wvo_psum, c + 1)
                        nc.scalar.activation(wvo32[:, c, :], banks[c][:, :], copy).then_inc(wvo_ready, 1)
                    act.wait_ge(aT_psum, 1)
                    nc.scalar.activation(aT, banks[0][0:RANK, :], copy).then_inc(aT_ready, 1)

            def Sx(a):
                act.wait_ge(scale_a, a.n // TILES + 2)
                act.wait_ge(x_in_loaded[a.par], (a.half + 1) * 16)
                nc.scalar.activation(x_in[a.par][:, :], x_in[a.par][:, :], copy, scale=sx
                                     ).then_inc(S["x_scaled"], 1)

            def Tx(a):
                act.wait_ge(S["xT_psum"], done(a.n))
                act.wait_ge(S["k_psum"], done(a.n - 2))
                nc.scalar.activation(xT[a.par][:, 0, :], TRANS[:, :], copy).then_inc(S["xTh"], 1)

            def Lk(a):
                act.wait_ge(S["k_psum"], done(a.n))
                if not a.first:
                    act.wait_ge(S["k_shifted"], done(a.n - TILES))
                slot = snapped(act, a.t * D)
                nc.scalar.activation(keys[:, ds(slot, D)], KEYS[:, :], copy).then_inc(S["k_stored"], 1)

            def Lq(a):
                act.wait_ge(S["x_scaled"], done(a.n))
                if not a.first:
                    act.wait_ge(S["g_psum"], done(a.n - TILES))
                slot = snapped(act, a.t * (2 * D))
                nc.scalar.activation(xn[:, ds(slot, D)], x_in[a.par][:, :], copy).then_inc(S["xnh"], 1)
                act.wait_ge(S["q_bias"], done(a.n))
                act.wait_ge(S["pT_psum"], done(a.n - 1))
                act.wait_ge(S["q_recip"], done(a.n - 1))
                nc.scalar.activation(exp_q[:, :], QUERIES[:, :], exp, bias=q_bias_c, scale=kq,
                                     accum_out=q_sum).then_inc(S["q_exp"], 1)

            def TP(a):
                act.wait_ge(S["pT_psum"], done(a.n))
                slot = snapped(act, a.ring * (2 * D))
                nc.scalar.activation(probs[:, ds(slot, D)], P_TRANS[:, :], copy, scale=PS).then_inc(S["pTh"], 1)

            def CB(b):
                act.wait_ge(kmax_row, b + 1)
                nc.scalar.activation(kshift[:, :], MISC[:, :], copy).then_inc(kshift_ready, 1)

            def exponentials(n, par):
                act.wait_ge(S["k_shifted"], done(n))
                nc.scalar.activation(exp_k[par][:, :], exp_k[par][:, :], exp, scale=kk).then_inc(S["k_exp"], 1)

            def E0(b):
                act.wait_ge(scale_b, b + 1)
                exponentials(b * TILES, 0)

            def B(k):
                if not (isinstance(k.t, int) and k.t == TILES - 1):
                    exponentials(k.n + 1, 1 - k.par)

            def GE(b):
                act.wait_ge(S["g_psum"], done(b * TILES + TILES - 1))
                for c in range(CH):
                    nc.scalar.activation(gt[:, 0, c, :], banks[c][:, :], copy, scale=GS).then_inc(gh, 1)

            def M(b, m):
                act.wait_ge(m_sum, b * CH + m + 1)
                nc.scalar.activation(attn[:, 0, m, :], exp_k[m % 2][:, :], copy).then_inc(mh, 1)

            def T1(c):
                act.wait_ge(S["x1T_psum"], done(c.n))
                act.wait_ge(S["ffn_psum"], done(c.n - 1))
                nc.scalar.activation(x1T[:, 0, :], X1T_BANK[:, :], copy, scale=NS).then_inc(S["x1Th"], 1)

            walk(act, {"setup": setup, "weights": weights, "Sx": Sx, "Tx": Tx, "Lk": Lk, "Lq": Lq, "TP": TP, "CB": CB, "E0": E0,
                       "B": B, "GE": GE, "M": M, "T1": T1})

        @block.vector
        def _(dve):
            V = nc.vector

            def power(dst, src, tmp, link):
                link(V.tensor_scalar(tmp, src, 1e-12, 1.0 / TOP, ALU.max, ALU.mult))
                link(V.reciprocal(tmp, tmp))
                link(V.tensor_scalar(dst.bitcast(i32), tmp.bitcast(i32), 0x7F800000, None, ALU.bitwise_and))

            chain = [0]

            def link_set(ins):
                chain[0] += 1
                ins.then_inc(dve_set, 1)
                dve.wait_ge(dve_set, chain[0])

            def absmax_of(k, w):
                return V.tensor_reduce(w_abs[:, k:k + 1], w, AX.XY, ALU.max, apply_absolute_value=True)

            def scale_of(k, src):
                power(sw[:, k:k + 1], w_abs_all[:, src:src + 1], t0, link_set)
                link_set(V.reciprocal(isw[:, k:k + 1], sw[:, k:k + 1]))

            def split(k, w32, w):
                link_set(V.tensor_scalar(w[:, 0], w32, sw[:, k:k + 1], None, ALU.mult))
                return V.scalar_tensor_tensor(w[:, 1], w32, sw[:, k:k + 1], w[:, 0], ALU.mult, ALU.subtract)

            def setup():
                dve.wait_ge(wq_loaded, 16)
                link_set(absmax_of(0, wq32))
                dve.wait_ge(wk_loaded, 16)
                absmax_of(1, wk32).then_inc(w_absmax, 1)
                V.memset(absmax_p, 0.0).then_inc(absmax_part, 1)
                link_set(V.memset(kmax[:, :], FAR))
                for name in names:
                    dve.sem_inc(S[name], LEAD)
                for k in range(2):
                    dve.sem_inc(out_stored[k], 16)
                dve.sem_inc(scale_a, 1)
                dve.sem_inc(setup_done, 1)
                dve.wait_ge(w_absmax_all, 1)
                for k, w32, w in ((0, wq32, wq), (1, wk32, wk)):
                    scale_of(k, k)
                    split(k, w32, w).then_inc(wqk_split, 1)

            def weights(k):
                big = 1.5 * 2.0 ** 23
                if k == 0:
                    dve.wait_ge(ffn_loaded, 16)
                    absmax_of(4, ffn32).then_inc(w_absmax, 1)
                if k == 1:
                    dve.wait_ge(w_absmax_all, 2)
                    link_set(V.tensor_scalar(t1, w_abs_all[:, 4:5], 1.0 / 7.0, None, ALU.mult))
                    link_set(V.reciprocal(t2, t1))
                    link_set(V.tensor_scalar(ffn32, ffn32, t2, big, ALU.mult, ALU.add))
                    link_set(V.tensor_scalar(ffn32, ffn32, big, -8.0, ALU.subtract, ALU.max))
                    link_set(V.tensor_scalar(ffn32, ffn32, 7.0, t1, ALU.min, ALU.mult))
                    dve.wait_ge(wvo_ready, CH)
                    link_set(absmax_of(3, wvo32))
                    dve.wait_ge(rows_all, 2)
                    link_set(V.tensor_reduce(bo_max, bo_all[:, :], AX.X, ALU.max, apply_absolute_value=True))
                if k == 2:
                    dve.wait_ge(ab_psum, CH)
                    dve.wait_ge(consts, 6)
                    for c in range(CH):
                        link_set(V.tensor_tensor(ffn32[:, c, :], ffn32[:, c, :], banks[c][:, :], ALU.add))
                        diag = ffn32[:, c, c * P:(c + 1) * P]
                        link_set(V.tensor_tensor(diag, diag, ident[:, :], ALU.add))
                    absmax_of(2, ffn32).then_inc(w_absmax, 1)
                if k == 3:
                    dve.wait_ge(w_absmax_all, 3)
                    for n, src, w32, w in ((2, 3, wvo32, wvo), (3, 2, ffn32, ffn)):
                        scale_of(n, src)
                        split(n, w32, w).then_inc(weights_split, 1)
                    link_set(V.tensor_scalar(b_attn, w_abs_all[:, 3:4], D * ATTN_SCALE, None, ALU.mult))
                    link_set(V.tensor_scalar(k_ffn, isw[:, 3:4], 1.0 / NS, None, ALU.mult))

            def X(x):
                dve.wait_ge(x_abs_loaded[x.q], (x.quad + 1) * 16)
                V.tensor_reduce(absmax_cols[:, ds(x.t, 1)], x_abs[x.q][:, :], AX.X, ALU.max,
                                apply_absolute_value=True).then_inc(S["x_absmax"], 1)

            def XS(s):
                dve.wait_ge(S["x_absmax"], done(s * TILES + TILES - 1))
                dve.wait_ge(absmax_all, s) if not (isinstance(s, int) and s == 0) else None
                V.tensor_reduce(absmax_p, absmax_cols[:, :], AX.X, ALU.max).then_inc(absmax_part, 1)

            def linker(sem_, start):
                at = [start]

                def link(ins):
                    at[0] = at[0] + 1
                    ins.then_inc(sem_, 1)
                    dve.wait_ge(sem_, at[0])
                return link

            def scale_a_(s):
                dve.wait_ge(absmax_all, s + 1)
                dve.wait_ge(S["x_scaled"], done(s * TILES - 1))
                dve.wait_ge(S["q_exp"], done(s * TILES - 1))
                link = linker(rot_a, s * ROT_A_STEPS)
                link(V.tensor_scalar(ax, absmax_new, 1.0, None, ALU.mult))
                power(sx, ax, t3, link)
                link(V.reciprocal(isx, sx))
                V.tensor_scalar(kq, isx, isw[:, 0:1], None, ALU.mult).then_inc(scale_a, 1)

            def scale_b_(b):
                dve.wait_ge(S["k_exp"], done(b * TILES - 1))
                dve.wait_ge(S["rq_scaled"], done(b * TILES - 1))
                link = linker(rot_b, b * ROT_STEPS)
                link(V.tensor_scalar(kk, isx, isw[:, 1:2], None, ALU.mult))
                link(V.tensor_scalar(t0, ax, b_attn, bo_max, ALU.mult, ALU.add))
                power(s_attn, t0, t1, link)
                link(V.tensor_scalar(t0, s_attn, PS, None, ALU.mult))
                link(V.reciprocal(g_attn, t0))
                link(V.tensor_scalar(t0, isx, isw[:, 2:3], ATTN_SCALE / (GS * PS), ALU.mult, ALU.mult))
                link(V.tensor_scalar(f_attn, t0, s_attn, None, ALU.mult))
                V.tensor_scalar(bo_scaled[:, :], bo_all[:, :], s_attn, None, ALU.mult).then_inc(scale_b, 1)

            def Tx(a):
                dve.wait_ge(S["xTh"], done(a.n))
                V.tensor_tensor(xT[a.par][:, 1, :], TRANS[:, :], xT[a.par][:, 0, :], ALU.subtract).then_inc(S["xTl"], 1)

            def Lk(a):
                dve.wait_ge(S["k_stored"], done(a.n))
                dve.wait_ge(S["k_max"], done(a.n - 1))
                if not a.first:
                    dve.wait_ge(kmax_reset, a.n // TILES)
                slot = snapped(dve, a.t * D)
                V.tensor_tensor(kmax[:, :], kmax[:, :], keys[:, ds(slot, D)], ALU.max).then_inc(S["k_max"], 1)

            def Lq(a):
                dve.wait_ge(S["q_psum"], done(a.n))
                V.tensor_reduce(q_rowmax_c, QUERIES[:, :], AX.X, ALU.max, negate=True).then_inc(S["q_rowmax"], 1)
                dve.wait_ge(S["q_rowmax"], done(a.n))
                dve.wait_ge(S["q_exp"], done(a.n - 1))
                V.tensor_scalar(q_bias_c, q_rowmax_c, kq, None, ALU.mult).then_inc(S["q_bias"], 1)

            def TP(a):
                dve.wait_ge(S["q_exp"], done(a.n))
                V.reciprocal(q_recip_all[:, ds(a.n, 1)], q_sum).then_inc(S["q_recip"], 1)
                dve.wait_ge(S["pTh"], done(a.n))
                slot = snapped(dve, a.ring * (2 * D))
                V.scalar_tensor_tensor(probs[:, ds(slot + D, D)], P_TRANS[:, :], PS, probs[:, ds(slot, D)],
                                       ALU.mult, ALU.subtract).then_inc(S["pTl"], 1)

            def CT(b):
                dve.wait_ge(kmaxT, b + 1)
                V.memset(kmax[:, :], FAR).then_inc(kmax_reset, 1)
                V.tensor_reduce(kmax_c, TRANS[:, :].rearrange("p (c n) -> p c n", c=CH), AX.X, ALU.max
                                ).then_inc(kmax_col, 1)
                dve.wait_ge(kmax_col, b + 1)
                V.tensor_tensor(exp_k[1][:, :].rearrange("p (c n) -> p c n", c=CH),
                                ident[:, :].unsqueeze(1).to_broadcast([P, CH, P]),
                                kmax_c.unsqueeze(2).to_broadcast([P, CH, P]), ALU.mult).then_inc(kmax_diag, 1)

            def split_e(n, par):
                dve.wait_ge(S["k_exp"], done(n))
                dve.wait_ge(S["g_psum"], done(n - 2))
                V.tensor_scalar(ek[par][:, 0, :], exp_k[par][:, :], PS, None, ALU.mult).then_inc(S["ekh"], 1)
                dve.wait_ge(S["ekh"], done(n))
                V.scalar_tensor_tensor(ek[par][:, 1, :], exp_k[par][:, :], PS, ek[par][:, 0, :],
                                       ALU.mult, ALU.subtract).then_inc(S["ek_split"], 1)

            def E0(b):
                split_e(b * TILES, 0)

            def B(k):
                if not (isinstance(k.t, int) and k.t == TILES - 1):
                    split_e(k.n + 1, 1 - k.par)

            def KS(b):
                dve.wait_ge(ksum_psum, b + 1)
                V.reciprocal(rk, MISC[:, 0:CH]).then_inc(ksum_recip, 1)
                dve.wait_ge(ksum_recip, b + 1)
                V.tensor_scalar(rkf, rk, f_attn, None, ALU.mult).then_inc(ksum_ready, 1)

            def GE(b):
                for c in range(CH):
                    dve.wait_ge(gh, b * CH + c + 1)
                    V.scalar_tensor_tensor(gt[:, 1, c, :], banks[c][:, :], GS, gt[:, 0, c, :],
                                           ALU.mult, ALU.subtract).then_inc(g_split, 1)

            def M(b, m):
                dve.wait_ge(m_psum, b * CH + m + 1)
                dve.wait_ge(ksum_ready, b + 1)
                if m < 2:
                    dve.wait_ge(S["k_summed"], done(b * TILES + TILES - 1))
                else:
                    dve.wait_ge(m_split, b * CH + m - 1)
                V.scalar_tensor_tensor(exp_k[m % 2][:, :], banks[m][:, :], rkf[:, m:m + 1], bo_scaled[:, :],
                                       ALU.mult, ALU.add).then_inc(m_sum, 1)

            def statistics(c, v, which, ln):
                V.bn_stats(stats[:, 2 * which + c.par, 0:6], v).then_inc(S["yz"[which] + "_stats"], 1)
                dve.wait_ge(S["yz"[which] + "_stats"], done(c.n))
                apart(dve)
                V.bn_aggr(stats[:, 2 * which + c.par, 6:8], stats[:, 2 * which + c.par, 0:6]
                          ).then_inc(S[ln + "_stats"], 1)

            def PM(c):
                dve.wait_ge(S["attn_psum"], done(c.n))
                dve.wait_ge(S["rq_scaled"], done(c.n))
                dve.wait_ge(y_loaded[c.q], (c.quad + 1) * 16)
                V.scalar_tensor_tensor(y[c.q][:, :], banks[c.par][:, :], rqg[c.par], y[c.q][:, :],
                                       ALU.mult, ALU.add).then_inc(S["y_sum"], 1)
                dve.wait_ge(S["y_sum"], done(c.n))
                statistics(c, y[c.q][:, :], 0, "ln1")

            def N1(c):
                dve.wait_ge(S["ln1_rstd"], done(c.n))
                V.tensor_scalar(y[c.q][:, :], y[c.q][:, :], stats[:, c.par, 6:7], rstd1[c.par],
                                ALU.subtract, ALU.mult).then_inc(S["x1_ready"], 1)

            def T1(c):
                dve.wait_ge(S["x1Th"], done(c.n))
                V.scalar_tensor_tensor(x1T[:, 1, :], X1T_BANK[:, :], NS, x1T[:, 0, :],
                                       ALU.mult, ALU.subtract).then_inc(S["x1T_split"], 1)

            def F(c):
                dve.wait_ge(S["ffn_psum"], done(c.n))
                dve.wait_ge(out_stored[c.par], (c.half + 1) * 16)
                V.scalar_tensor_tensor(z[c.par][:, :], FFN_BANK[:, :], k_ffn, bias_all[:, :],
                                       ALU.mult, ALU.add).then_inc(S["z_sum"], 1)
                dve.wait_ge(S["z_sum"], done(c.n))
                statistics(c, z[c.par][:, :], 1, "ln2")

            def N2(c):
                dve.wait_ge(S["ln2_rstd"], done(c.n))
                V.tensor_scalar(z[c.par][:, :], z[c.par][:, :], stats[:, 2 + c.par, 6:7], rstd2[c.par],
                                ALU.subtract, ALU.mult).then_inc(S["out_ready"], 1)

            walk(dve, {"setup": setup, "weights": weights, "X": X, "XS": XS, "scale_a": scale_a_, "scale_b": scale_b_, "Tx": Tx,
                       "Lk": Lk, "Lq": Lq, "TP": TP, "CT": CT, "E0": E0, "B": B, "KS": KS, "GE": GE, "M": M, "PM": PM,
                       "N1": N1, "T1": T1, "F": F, "N2": N2})

        @block.tensor
        def _(pe):
            mm = nc.tensor.matmul

            def chunk(c):
                return slice(c * P, (c + 1) * P)

            def transposes(bank, src):
                for c in range(CH):
                    last = nc.tensor.transpose(bank[:, chunk(c)], src[:, chunk(c)], ident[:, :])
                return last

            def split_product(bank, left, right, start=True, stop=True):
                for c in range(CH):
                    mm(bank, left(0, c), right(0, c), start=start and c == 0, stop=False)
                    mm(bank, left(0, c), right(1, c), start=False, stop=False)
                    last = mm(bank, left(1, c), right(0, c), start=False, stop=stop and c == CH - 1)
                return last

            def setup():
                pe.wait_ge(consts, 6)
                for k, (bank, row, there) in enumerate(((KEYS, bo_row, bo_loaded), (QUERIES, bias_row, bias_loaded))):
                    pe.wait_ge(there, 16)
                    mm(bank[:, :], ones[0:1, :], row, start=True, stop=True).then_inc(rows_psum, 1)
                pe.wait_ge(rows_all, 2)
                pe.wait_ge(wqk_split, 2)
                pe.wait_ge(setup_done, 1)

            def weights(k):
                if k == 0:
                    pe.wait_ge(wv_loaded, 16)
                    for m in range(CH):
                        for c in range(CH):
                            last = nc.tensor.transpose(banks[m][:, chunk(c)], wv32[:, c, chunk(m)], ident[:, :])
                        last.then_inc(wv_psum, 1)
                if k == 1:
                    pe.wait_ge(wo_loaded, 16)
                    pe.wait_ge(wvT_ready, CH)
                    for c in range(CH):
                        for m in range(CH):
                            last = mm(banks[c][:, :], wvT[:, m, chunk(c)], wo32[:, m, :],
                                      start=m == 0, stop=m == CH - 1)
                        last.then_inc(wvo_psum, 1)
                    pe.wait_ge(a_loaded, 16)
                    pe.wait_ge(wvo_ready, 1)
                    for c in range(CH):
                        last = nc.tensor.transpose(banks[0][0:RANK, chunk(c)], a32[:, c * RANK:(c + 1) * RANK],
                                                   ident[:, :])
                    last.then_inc(aT_psum, 1)
                if k == 2:
                    pe.wait_ge(b_loaded, 16)
                    pe.wait_ge(aT_ready, 1)
                    pe.wait_ge(wvo_ready, CH)
                    for c in range(CH):
                        mm(banks[c][:, :], aT[:, chunk(c)], b32, start=True, stop=True).then_inc(ab_psum, 1)

            def Tx(a):
                pe.wait_ge(S["x_scaled"], done(a.n))
                pe.wait_ge(S["xTl"], done(a.n - 1))
                transposes(TRANS, x_in[a.par]).then_inc(S["xT_psum"], 1)

            def from_x(a):
                return lambda part, c: xT[a.par][:, part, chunk(c)]

            def Lk(a):
                pe.wait_ge(S["k_stored"], done(a.n - 1))
                split_product(KEYS[:, :], from_x(a), lambda part, c: wk[:, part, c, :]).then_inc(S["k_psum"], 1)

            def Lq(a):
                pe.wait_ge(S["xTl"], done(a.n))
                pe.wait_ge(S["q_exp"], done(a.n - 1))
                split_product(QUERIES[:, :], from_x(a), lambda part, c: wq[:, part, c, :]).then_inc(S["q_psum"], 1)

            def TP(a):
                pe.wait_ge(S["q_exp"], done(a.n))
                pe.wait_ge(S["pTl"], done(a.n - 1))
                if isinstance(a.t, int) and a.t == 7 and not a.first:
                    pe.wait_ge(ksum_recip, a.n // TILES)
                transposes(P_TRANS, exp_q).then_inc(S["pT_psum"], 1)

            def CT(b):
                pe.wait_ge(S["k_max"], done(b * TILES + TILES - 1))
                pe.wait_ge(S["xTl"], done(b * TILES + TILES - 1))
                transposes(TRANS, kmax).then_inc(kmaxT, 1)

            def CB(b):
                pe.wait_ge(kmax_diag, b + 1)
                pe.wait_ge(S["pTl"], done(b * TILES + TILES - 1))
                mm(MISC[:, :], ones[:, :], exp_k[1][:, :], start=True, stop=True).then_inc(kmax_row, 1)

            def clear(b):
                pe.wait_ge(weights_split, 2)
                pe.wait_ge(S["z_sum"], done(b * TILES - 1))
                pe.wait_ge(S["y_sum"], done(b * TILES - 1))
                for c in range(CH):
                    mm(banks[c][:, :], zeros[:, :], wq[:, 0, 0, :], start=True, stop=False)

            def B(k):
                pe.wait_ge(S["ek_split"], done(k.n))
                pe.wait_ge(S["xn_split"], done(k.n))
                slot = snapped(pe, k.t * (2 * D))
                end = isinstance(k.t, int) and k.t == TILES - 1
                for c in range(CH):
                    high = xn[:, ds(slot + c * P, P)]
                    low = xn[:, ds(slot + (D + c * P), P)]
                    mm(banks[c][:, :], high, ek[k.par][:, 0, :], start=False, stop=False)
                    mm(banks[c][:, :], high, ek[k.par][:, 1, :], start=False, stop=False)
                    last = mm(banks[c][:, :], low, ek[k.par][:, 0, :], start=False, stop=end)
                last.then_inc(S["g_psum"], 1)

            def KS(b):
                pe.wait_ge(S["k_summed"], done(b * TILES + TILES - 1))
                pe.wait_ge(S["pTl"], done(BATCHES * TILES - 1 if isinstance(b, int) else (b + 1) * TILES + 6))
                for c in range(CH):
                    last = mm(MISC[:, c:c + 1], ksum[:, chunk(c)], ones[:, 0:1], start=True, stop=True)
                last.then_inc(ksum_psum, 1)

            def M(b, m):
                pe.wait_ge(g_split, b * CH + CH)
                split_product(banks[m][:, :], lambda part, c: gt[:, part, c, chunk(m)],
                              lambda part, c: wvo[:, part, c, :]).then_inc(m_psum, 1)

            def PM(c):
                pe.wait_ge(m_split, (c.quad // (TILES // 4) + 1) * CH)
                pe.wait_ge(S["pTl"], done(c.n))
                pe.wait_ge(S["y_sum"], done(c.n - 2))
                slot = snapped(pe, c.ring * (2 * D))
                split_product(banks[c.par][:, :], lambda part, k: probs[:, ds(slot + (part * D + k * P), P)],
                              lambda part, k: attn[:, part, k, :]).then_inc(S["attn_psum"], 1)

            def T1(c):
                pe.wait_ge(S["x1_ready"], done(c.n))
                pe.wait_ge(S["x1T_split"], done(c.n - 1))
                transposes(X1T_BANK, y[c.q]).then_inc(S["x1T_psum"], 1)

            def F(c):
                pe.wait_ge(S["x1T_split"], done(c.n))
                pe.wait_ge(S["z_sum"], done(c.n - 1))
                split_product(FFN_BANK[:, :], lambda part, k: x1T[:, part, chunk(k)],
                              lambda part, k: ffn[:, part, k, :]).then_inc(S["ffn_psum"], 1)

            walk(pe, {"setup": setup, "Tx": Tx, "Lk": Lk, "Lq": Lq, "TP": TP, "CT": CT, "CB": CB, "B": B, "weights": weights,
                      "clear": clear, "KS": KS, "M": M, "PM": PM, "T1": T1, "F": F})


_INS = {"x": "L0_attn_x", "Wq": "L0_attn_Wq", "Wk": "L0_attn_Wk", "Wv": "L0_attn_Wv", "Wo": "L0_attn_Wo",
        "bo": "L0_attn_bo", "kernel": "L0_ffn_kernel", "bias": "L0_ffn_bias", "lora_a": "L0_ffn_a",
        "lora_b": "L0_ffn_b"}


def kernel(**inputs):
    import numpy as np
    import concourse.bacc as bacc
    from concourse.bass_utils import run_bass_kernel_spmd

    nc = bacc.Bacc("TRN2", target_bir_lowering=False, num_devices=1, dynamic_dma_scratch_size=4096)
    arrays, args = {}, {}
    for arg, name in _INS.items():
        a = np.ascontiguousarray(inputs[name])
        arrays[f"in_{arg}"] = a
        args[arg] = nc.dram_tensor(f"in_{arg}", a.shape, mybir.dt.from_np(a.dtype), kind="ExternalInput").ap()
    shape = (BATCHES, TOKENS, D)
    args["out"] = nc.dram_tensor("out_dram", shape, mybir.dt.float32, kind="ExternalOutput").ap()
    build(nc, **args)
    r = run_bass_kernel_spmd(nc, [arrays], core_ids=[0])
    return r.results[0]["out_dram"]
```

```python
import concourse.bass as bass
from concourse import mybir
from contextlib import ExitStack


P = 128
BATCHES, TOKENS, D = 8, 2048, 512
RANK = 16
CH = D // P
TILES = TOKENS // P
RING = 24
LEAD = 4
EPS = 1e-5
ATTN_SCALE = 1.0 / (D // 16) ** 0.5 / D
FAR = -3.0e38
PS = 4096.0
NS = 512.0
GS = 2.0 ** -22
TOP = 2.0 ** 13
TURN_LINKS, NEXT_LINKS = 9, 5


def done(n):
    return n + 1 + LEAD


class Tile:

    def __init__(self, n, t, half, quad, q, ring, first=False):
        self.first = first
        self.n, self.t, self.half, self.quad, self.q, self.ring = n, t, half, quad, q, ring
        self.par = q % 2


def snapped(eng, value):
    return value if isinstance(value, int) else eng.snap(value)


def pair(eng, p, t, first=False):
    p = snapped(eng, p)
    n, ring = snapped(eng, p * 2), snapped(eng, p % (RING // 2) * 2)
    return [Tile(n + k, t + k, p, None, k, ring + k, first) for k in range(2)]


def quad(eng, p, t, first=False):
    p = snapped(eng, p)
    n, ring = snapped(eng, p * 4), snapped(eng, p % (RING // 4) * 4)
    return [Tile(n + k, t + k, p * 2 + k // 2, p, k, ring + k, first) for k in range(4)]


def walk(eng, do):

    def step(name, *args):
        if name in do:
            do[name](*args)

    step("setup")
    step("XS", 0)
    step("scale_next", 0)
    step("turn_a", 0)

    def a_alone(a, following, x):
        if following is not None:
            step("Sx", following)
        step("Lq", a)
        if following is not None:
            step("Tx", following)
        step("X", x)
        step("Lk", a)
        step("TP", a)

    per = TILES // 4

    def a_quad(g, ends=False):
        a = quad(eng, g, g * 4, True)
        a.append(None if ends else quad(eng, g + 1, g * 4 + 4, True)[0])
        return a, quad(eng, g + per, g * 4)

    a, _ = a_quad(0)
    step("Sx", a[0])
    step("Tx", a[0])
    for g in range(per - 2):
        a, x = a_quad(g)
        for k in range(4):
            a_alone(a[k], a[k + 1], x[k])
            step("weights", 4 * g + k)
    with eng.Fori(per - 2, per - 1) as g:
        a, x = a_quad(g)
        for k in range(4):
            a_alone(a[k], a[k + 1], x[k])
    a, x = a_quad(per - 1, ends=True)
    for k in range(4):
        a_alone(a[k], a[k + 1], x[k])
        step("weights", TILES // 2 + k)
        if k == 2:
            step("turn_b", 0)
    step("XS", 1)
    step("CT", 0)
    step("CM", 0)
    step("clear", 0)
    step("scale_next", 1)
    step("turn_a", 1)
    step("CB", 0)
    a = pair(eng, TILES // 2, 0)
    step("Sx", a[0])
    step("Tx", a[0])
    step("E0", 0)

    def period(b, last):

        def a_tiles(i, odd=0):
            if last:
                return [None] * 3
            both = pair(eng, (b + 1) * (TILES // 2) + i, i * 2) + pair(eng, (b + 1) * (TILES // 2) + i + 1, i * 2 + 2)
            return both[odd:odd + 3]

        def a_step(name, a):
            if not last and a is not None:
                step(name, a)

        def b_unit(a, following, bs, xs):
            step("B", bs[0])
            a_step("Sx", following)
            a_step("Lq", a)
            a_step("Tx", following)
            a_step("X", xs[0])
            step("B", bs[1])
            a_step("Lk", a)
            a_step("X", xs[1])
            a_step("TP", a)

        def quads(i):
            return quad(eng, b * per + i, i * 4), [None] * 4 if last else quad(eng, (b + 2) * per + i, i * 4)

        with eng.Fori(0, 3) as g:
            a = a_tiles(g)
            bs, xs = quads(g)
            b_unit(a[0], a[1], bs[0:2], xs[0:2])
            b_unit(a[1], a[2], bs[2:4], xs[2:4])
        a = a_tiles(3)
        bs, xs = quads(3)
        b_unit(a[0], a[1], bs[0:2], xs[0:2])
        step("B", bs[2])
        a_step("Sx", a[2])
        a_step("Lq", a[1])
        a_step("Tx", a[2])
        a_step("X", xs[2])
        step("B", bs[3])
        a_step("X", xs[3])
        step("KS", b)
        step("GE", b)
        a_step("Lk", a[1])
        step("M", b, 0)
        a_step("TP", a[1])
        step("M", b, 1)
        step("M", b, 2)
        step("M", b, 3)
        a_step("XS", b + 2)
        a_step("turn_b", b + 1)
        a = a_tiles(4)
        a_step("Sx", a[1])
        a_step("Lq", a[0])
        a_step("Tx", a[1])
        a_step("Lk", a[0])
        cs = quad(eng, b * per, 0)
        step("PM", cs[0])
        step("N1", cs[0])
        step("PM", cs[1])
        a_step("TP", a[0])
        step("T1", cs[0])
        a_step("scale_next", b + 2)

        def c_unit(a, following, c, ahead, batch_ends=False):
            a_step("Sx", following)
            a_step("Lq", a)
            step("N1", c[1])
            step("PM", ahead[0])
            step("F", c[0])
            step("FS", c[0])
            step("R2", c[0])
            a_step("Tx", following)
            step("T1", c[1])
            a_step("Lk", a)
            step("N2", c[0])
            step("N1", ahead[0])
            step("PM", ahead[1])
            a_step("TP", a)
            if batch_ends:
                step("N1", ahead[1])
                a_step("CT", b + 1)
                step("T1", ahead[0])
                a_step("CM", b + 1)
                step("F", c[1])
                step("FS", c[1])
                step("R2", c[1])
                step("T1", ahead[1])
            else:
                step("F", c[1])
                step("FS", c[1])
                step("R2", c[1])
                step("T1", ahead[0])
                step("N2", c[1])

        with eng.Fori(0, 3) as g:
            a = a_tiles(g + 4, 1)
            cs = quad(eng, b * per + g, g * 4)
            ahead = quad(eng, b * per + g + 1, g * 4 + 4)
            c_unit(a[0], a[1], cs[0:2], cs[2:4])
            c_unit(a[1], a[2], cs[2:4], ahead[0:2])
        a = a_tiles(7, 1)
        cs = quad(eng, b * per + 3, 12)
        c_unit(a[0], None, cs[0:2], cs[2:4], batch_ends=True)
        a_step("turn_a", b + 2)
        step("N2", cs[1])
        a = None if last else pair(eng, (b + 2) * (TILES // 2), 0)[0]
        step("F", cs[2])
        a_step("CB", b + 1)
        a_step("Sx", a)
        step("FS", cs[2])
        step("R2", cs[2])
        step("F", cs[3])
        a_step("E0", b + 1)
        step("N2", cs[2])
        step("FS", cs[3])
        step("R2", cs[3])
        a_step("Tx", a)
        step("N2", cs[3])
        a_step("clear", b + 1)

    with eng.Fori(0, BATCHES - 1) as b:
        period(b, False)
    period(BATCHES - 1, True)


def build(nc, x, Wq, Wk, Wv, Wo, bo, kernel, bias, lora_a, lora_b, out):
    fp32, fp16, i32 = mybir.dt.float32, mybir.dt.float16, mybir.dt.int32
    ALU, ACT, AX = mybir.AluOpType, mybir.ActivationFunctionType, mybir.AxisListType
    ds = bass.ds

    x_rows = x.rearrange("b n d -> (b n) d")
    out_rows = out.rearrange("b n d -> (b n) d")

    ctx = ExitStack()
    with ctx:
        def sb(name, shape, dt):
            return ctx.enter_context(nc.sbuf_tensor(name, shape, dt))

        def sem(name):
            return ctx.enter_context(nc.semaphore(name))

        wq = sb("wq", [P, 2, CH, D], fp16)
        wk = sb("wk", [P, 2, CH, D], fp16)
        wvo = sb("wvo", [P, 2, CH, D], fp16)
        ffn = sb("ffn", [P, 2, CH, D], fp16)
        attn = sb("attn", [P, 2, CH, D], fp16)
        gt = sb("gt", [P, 2, CH, D], fp16)
        probs = sb("probs", [P, RING * 2 * D], fp16)
        keys = sb("keys", [P, TILES * D], fp32)
        xn = sb("xn", [P, TILES * 2 * D], fp16)
        x_in = [sb(f"x_in{i}", [P, D], fp32) for i in range(2)]
        x_abs = [sb(f"x_abs{i}", [P, D], fp32) for i in range(4)]
        xT = [sb(f"xT{i}", [P, 2, D], fp16) for i in range(2)]
        exp_q = sb("exp_q", [P, D], fp32)
        exp_k = [sb(f"exp_k{i}", [P, D], fp32) for i in range(2)]
        ek = [sb(f"ek{i}", [P, 2, D], fp16) for i in range(2)]
        kmax = sb("kmax", [P, D], fp32)
        ksum = sb("ksum", [P, D], fp32)
        kshift = sb("kshift", [P, D], fp32)
        bo_all = sb("bo_all", [P, D], fp32)
        bo_scaled = sb("bo_scaled", [P, D], fp32)
        bias_all = sb("bias_all", [P, D], fp32)
        y = [sb(f"y{i}", [P, D], fp32) for i in range(4)]
        x1T = [sb(f"x1T{i}", [P, 2, D], fp16) for i in range(2)]
        z = [sb(f"z{i}", [P, D], fp32) for i in range(2)]
        ident = sb("ident", [P, P], fp32)
        ones = sb("ones", [P, P], fp32)
        zeros = sb("zeros", [P, P], fp16)
        q_recip_all = sb("q_recip_all", [P, BATCHES * TILES], fp32)
        absmax_cols = sb("absmax_cols", [P, TILES], fp32)
        stats = sb("stats", [P, 4, 8], fp32)
        x0 = probs[:, 0:TILES * 2 * D].bitcast(fp32)

        def matrix(t):
            return t.rearrange("p (c n) -> p c n", c=CH)

        wq32, wk32, ab32 = (matrix(keys[:, k * CH * D:(k + 1) * CH * D]) for k in range(3))
        late = probs[:, TILES * 2 * D:RING * 2 * D].bitcast(fp32)
        ffn32, wo32 = matrix(late[:, 0:CH * D]), matrix(late[:, CH * D:2 * CH * D])
        wv32 = matrix(gt[:, :, :, :].rearrange("p h c n -> p (h c n)").bitcast(fp32))
        wvo32 = wv32
        wvT = matrix(attn[:, :, :, :].rearrange("p h c n -> p (h c n)").bitcast(fp32))
        a32, aT, b32 = z[0][:, 0:CH * RANK], z[1][0:RANK, :], exp_k[0][0:RANK, :]
        bo_row, bias_row = exp_k[1][0:1, :], kshift[0:1, :]

        def column(name, k=1):
            return sb(name, [P, k], fp32)[:, :]

        sx, sx_next, isx, ax = column("sx"), column("sx_next"), column("isx"), column("ax")
        kq, kq_next, kk = column("kq"), column("kq_next"), column("kk")
        s_attn, f_attn = column("s_attn"), column("f_attn")
        g_attn = column("g_attn", 2)
        k_ffn = column("k_ffn")
        sw, isw = column("sw", 4), column("isw", 4)
        b_attn, bo_max = column("b_attn"), column("bo_max")
        w_abs, w_abs_all = column("w_abs", 5), column("w_abs_all", 5)
        absmax_p, absmax_new = column("absmax_p"), column("absmax_new")
        q_sum, q_rowmax_c, q_bias_c = column("q_sum"), column("q_rowmax_c"), column("q_bias_c")
        rk, rkf, kmax_c = column("rk", CH), column("rkf", CH), column("kmax_c", CH)
        half_neg = column("half_neg")
        t01, t2, t3 = column("t01", 2), column("t2"), column("t3")
        t0, t1 = t01[:, 0:1], t01[:, 1:2]
        rqg, rstd1, rstd2 = ([column(f"{n}{i}") for i in range(2)] for n in ("rqg", "rstd1_", "rstd2_"))

        banks = [ctx.enter_context(nc.psum_tensor(f"bank{i}", [P, D], fp32)) for i in range(8)]
        TRANS, KEYS, QUERIES, MISC = banks[4:8]
        P_TRANS = MISC

        def is_tile(c, t):
            return isinstance(c.t, int) and c.t == t

        def x1T_bank(c):
            return banks[1] if is_tile(c, TILES - 1) else banks[2]

        def ffn_bank(c):
            return banks[0] if is_tile(c, TILES - 2) else banks[3]

        names = """x_scaled xT_psum xTh xTl k_psum q_psum k_stored k_max q_rowmax q_bias q_exp q_recip
            pT_psum pTh pTl xnh xn_split x_absmax k_shifted k_exp ekh ek_split k_summed g_psum
            rq_scaled attn_psum y_sum y_stats ln1_stats ln1_var ln1_rstd x1_ready x1T_psum x1Th x1T_split
            ffn_psum z_sum z_stats ln2_stats ln2_var ln2_rstd out_ready""".split()
        S = {name: sem(name) for name in names}
        x_in_loaded = [sem(f"x_in_loaded{i}") for i in range(2)]
        x_abs_loaded = [sem(f"x_abs_loaded{i}") for i in range(4)]
        y_loaded = [sem(f"y_loaded{i}") for i in range(4)]
        out_stored = [sem(f"out_stored{i}") for i in range(2)]
        kmaxT, kmax_col, kmax_reset, kmax_spread, kmax_row, kshift_ready = (sem(n) for n in (
            "kmaxT", "kmax_col", "kmax_reset", "kmax_spread", "kmax_row", "kshift_ready"))
        ksum_psum, ksum_recip, ksum_ready, ksum_reset = (sem(n) for n in (
            "ksum_psum", "ksum_recip", "ksum_ready", "ksum_reset"))
        gh, g_split, m_psum, m_sum, mh, m_split = (sem(n) for n in (
            "gh", "g_split", "m_psum", "m_sum", "mh", "m_split"))
        absmax_part, absmax_all, scale_next, scale_a, scale_b = (sem(n) for n in (
            "absmax_part", "absmax_all", "scale_next", "scale_a", "scale_b"))
        next_link, turn_link = sem("next_link"), sem("turn_link")
        wq_loaded, wk_loaded, wv_loaded, wo_loaded, ffn_loaded, a_loaded, b_loaded, bo_loaded, bias_loaded = (
            sem(n) for n in ("wq_loaded", "wk_loaded", "wv_loaded", "wo_loaded", "ffn_loaded", "a_loaded",
                             "b_loaded", "bo_loaded", "bias_loaded"))
        rows_psum, rows_all, wv_psum, wvT_ready, aT_psum, aT_ready, wvo_psum, wvo_ready, ab_psum = (
            sem(n) for n in ("rows_psum", "rows_all", "wv_psum", "wvT_ready", "aT_psum", "aT_ready", "wvo_psum",
                             "wvo_ready", "ab_psum"))
        consts, dve_set, w_absmax, w_absmax_all, w_split, ab_ready = (
            sem(n) for n in ("consts", "dve_set", "w_absmax", "w_absmax_all", "w_split", "ab_ready"))
        x0_loaded = [sem(f"x0_loaded{k}") for k in range(TILES // 4)]
        w_scale, w_scaled, w_high = sem("w_scale"), sem("w_scaled"), sem("w_high")
        leads_set, waited = sem("leads_set"), sem("waited")

        def apart(eng):
            eng.sem_inc(waited, 1)

        block = ctx.enter_context(nc.Block())

        @block.sync
        def _(sp):
            def setup():
                for row, src, there in ((bo_row, bo, bo_loaded), (bias_row, bias, bias_loaded)):
                    sp.dma_start(row, src.rearrange("(a n) -> a n", a=1)).then_inc(there, 16)
                sp.dma_start(a32.rearrange("p (c r) -> p c r", c=CH),
                             lora_a.rearrange("(c p) r -> p c r", p=P)).then_inc(a_loaded, 16)
                sp.dma_start(b32, lora_b).then_inc(b_loaded, 16)
                for dst, w, there in ((wv32, Wv, wv_loaded), (wo32, Wo, wo_loaded), (wq32, Wq, wq_loaded),
                                      (wk32, Wk, wk_loaded)):
                    sp.dma_start(dst, w.rearrange("(c p) n -> p c n", p=P)).then_inc(there, 16)
                for k in range(TILES // 4):
                    cols = slice(k * 4 * D, (k + 1) * 4 * D)
                    sp.dma_start(x0[:, cols].rearrange("p (t d) -> p t d", t=4),
                                 x_rows[k * 4 * P:(k + 1) * 4 * P, :].rearrange("(t p) d -> p t d", p=P)
                                 ).then_inc(x0_loaded[k], 16)
                sp.wait_ge(leads_set, 1)

            def XS(s):
                if not (isinstance(s, int) and s == 0):
                    return
                for k in range(2):
                    sp.dma_start(x_in[k][:, :], x_rows[k * P:(k + 1) * P, :]).then_inc(x_in_loaded[k], 16)
                sp.dma_start(ffn32, kernel.rearrange("(c p) n -> p c n", p=P)).then_inc(ffn_loaded, 16)
                for q in range(4):
                    sp.dma_start(y[q][:, :], x_rows[q * P:(q + 1) * P, :]).then_inc(y_loaded[q], 16)

            def X(x):
                sp.wait_ge(S["x_absmax"], done(x.n - 4))
                row = snapped(sp, x.n % (BATCHES * TILES) * P)
                sp.dma_start(x_abs[x.q][:, :], x_rows[ds(row, P), :]).then_inc(x_abs_loaded[x.q], 16)

            def Lk(a):
                sp.wait_ge(S["xn_split"], done(a.n))
                sp.wait_ge(S["xT_psum"], done(a.n))
                row = snapped(sp, (a.n + 2) % (BATCHES * TILES) * P)
                sp.dma_start(x_in[a.par][:, :], x_rows[ds(row, P), :]).then_inc(x_in_loaded[a.par], 16)

            def T1(c):
                if isinstance(c.n, int) and c.n + 4 >= BATCHES * TILES:
                    return
                sp.wait_ge(S["x1T_psum"], done(c.n))
                row = snapped(sp, (c.n + 4) % (BATCHES * TILES) * P)
                sp.dma_start(y[c.q][:, :], x_rows[ds(row, P), :]).then_inc(y_loaded[c.q], 16)

            def N2(c):
                sp.wait_ge(S["out_ready"], done(c.n))
                row = snapped(sp, c.n * P)
                sp.dma_start(out_rows[ds(row, P), :], z[c.par][:, :]).then_inc(out_stored[c.par], 16)

            walk(sp, {"setup": setup, "XS": XS, "X": X, "Lk": Lk, "T1": T1, "N2": N2})
            for k in range(2):
                sp.wait_ge(out_stored[k], 16 * (BATCHES * TILES // 2 + 1))

        @block.gpsimd
        def _(pool):
            def setup():
                nc.gpsimd.memset(ident[:, :], 0.0).then_inc(consts, 1)
                nc.gpsimd.memset(ones[:, :], 1.0).then_inc(consts, 1)
                nc.gpsimd.memset(zeros[:, :], 0.0).then_inc(consts, 1)
                nc.gpsimd.memset(half_neg, -0.5).then_inc(consts, 1)
                nc.gpsimd.memset(ksum[:, :], 0.0).then_inc(consts, 1)
                pool.wait_ge(consts, 5)
                nc.gpsimd.affine_select(out=ident[:, :], in_=ident[:, :], compare_op=ALU.not_equal, fill=1.0,
                                        base=0, pattern=[[-1, P]], channel_multiplier=1).then_inc(consts, 1)
                largest(0, 0, 2)
                pool.wait_ge(leads_set, 1)
                low(0, wq32, wq)

            def low(k, w32, w):
                pool.wait_ge(w_high, k + 1)
                nc.gpsimd.tensor_tensor(w[:, 1], w32, w[:, 0], ALU.subtract).then_inc(w_split, 1)

            def largest(k, lo, hi):
                pool.wait_ge(w_absmax, k + 1)
                nc.gpsimd.partition_all_reduce(w_abs_all[:, lo:hi], w_abs[:, lo:hi], P,
                                               bass.bass_isa.ReduceOp.absmax).then_inc(w_absmax_all, 1)

            def weights(k):
                if k == 0:
                    largest(1, 4, 5)
                if k == 7:
                    largest(2, 2, 4)
                if k == 9:
                    low(2, wvo32, wvo)
                if k == 10:
                    low(3, ffn32, ffn)

            def XS(s):
                pool.wait_ge(absmax_part, s + 2)
                if not (isinstance(s, int) and s == 0):
                    pool.wait_ge(scale_next, s)
                apart(pool)
                nc.gpsimd.partition_all_reduce(absmax_new, absmax_p, P, bass.bass_isa.ReduceOp.absmax
                                               ).then_inc(absmax_all, 1)
                if isinstance(s, int) and s == 0:
                    low(1, wk32, wk)

            def Lk(a):
                pool.wait_ge(S["xnh"], done(a.n))
                slot = snapped(pool, a.t * (2 * D))
                nc.gpsimd.tensor_tensor(xn[:, ds(slot + D, D)], x_in[a.par][:, :], xn[:, ds(slot, D)], ALU.subtract
                                        ).then_inc(S["xn_split"], 1)

            def shift(n, t, par):
                pool.wait_ge(S["ek_split"], done(n - 2))
                pool.wait_ge(S["k_summed"], done(n - 2))
                slot = snapped(pool, t * D)
                nc.gpsimd.tensor_tensor(exp_k[par][:, :], keys[:, ds(slot, D)], kshift[:, :], ALU.subtract
                                        ).then_inc(S["k_shifted"], 1)

            def CT(b):
                pool.wait_ge(kmaxT, b + 1)
                apart(pool)
                nc.gpsimd.memset(kmax[:, :], FAR).then_inc(kmax_reset, 1)

            def CB(b):
                pool.wait_ge(kshift_ready, b + 1)
                shift(b * TILES, 0, 0)
                shift(b * TILES + 1, 1, 1)

            def B(k):
                pool.wait_ge(S["k_exp"], done(k.n))
                pool.wait_ge(S["k_summed"], done(k.n - 1))
                nc.gpsimd.tensor_tensor(ksum[:, :], ksum[:, :], exp_k[k.par][:, :], ALU.add
                                        ).then_inc(S["k_summed"], 1)
                if not (isinstance(k.t, int) and k.t >= TILES - 2):
                    shift(k.n + 2, k.t + 2, k.par)

            def KS(b):
                pool.wait_ge(ksum_psum, b + 1)
                apart(pool)
                nc.gpsimd.memset(ksum[:, :], 0.0).then_inc(ksum_reset, 1)

            def M(b, m):
                pool.wait_ge(mh, b * CH + m + 1)
                nc.gpsimd.tensor_tensor(attn[:, 1, m, :], exp_k[m % 2][:, :], attn[:, 0, m, :], ALU.subtract
                                        ).then_inc(m_split, 1)

            def PM(c):
                pool.wait_ge(S["q_recip"], done(c.n))
                pool.wait_ge(scale_b, c.quad // (TILES // 4) + 1)
                pool.wait_ge(S["y_sum"], done(c.n - 2))
                parity = snapped(pool, c.quad // (TILES // 4) % 2)
                nc.gpsimd.tensor_tensor(rqg[c.par], q_recip_all[:, ds(c.n, 1)], g_attn[:, ds(parity, 1)], ALU.mult
                                        ).then_inc(S["rq_scaled"], 1)
                rstd(c, 0, rstd1, "ln1")

            def rstd(c, which, dst, ln):
                pool.wait_ge(S[ln + "_stats"], done(c.n))
                mv = stats[:, 2 * which + c.par, 6:8]
                apart(pool)
                nc.gpsimd.tensor_scalar(mv[:, 1:2], mv[:, 1:2], EPS, 1.0, ALU.add, ALU.mult
                                        ).then_inc(S[ln + "_var"], 1)
                pool.wait_ge(S[ln + "_var"], done(c.n))
                nc.gpsimd.tensor_tensor(dst[c.par], mv[:, 1:2], half_neg, ALU.pow).then_inc(S[ln + "_rstd"], 1)

            def R2(c):
                rstd(c, 1, rstd2, "ln2")

            walk(pool, {"setup": setup, "weights": weights, "XS": XS, "Lk": Lk, "CT": CT, "CB": CB, "B": B, "KS": KS,
                        "M": M, "PM": PM, "R2": R2})

        @block.scalar
        def _(act):
            copy, exp = ACT.Copy, ACT.Exp

            def setup():
                for k, (dst, bank) in enumerate(((bo_all, KEYS), (bias_all, QUERIES))):
                    act.wait_ge(rows_psum, k + 1)
                    nc.scalar.activation(dst[:, :], bank[:, :], copy).then_inc(rows_all, 1)
                act.wait_ge(leads_set, 1)
                for m in range(CH):
                    act.wait_ge(wv_psum, m + 1)
                    nc.scalar.activation(wvT[:, m, :], banks[m][:, :], copy).then_inc(wvT_ready, 1)
                act.wait_ge(aT_psum, 1)
                nc.scalar.activation(aT, TRANS[0:RANK, :], copy).then_inc(aT_ready, 1)
                act.wait_ge(w_scale, 1)
                for k, (w32, w) in enumerate(((wq32, wq), (wk32, wk))):
                    nc.scalar.activation(w32, w32, copy, scale=sw[:, k:k + 1]).then_inc(w_scaled, 1)
                    high(k, w32, w)
                for c in range(CH):
                    act.wait_ge(ab_psum, c + 1)
                    nc.scalar.activation(ab32[:, c, :], banks[4 + c][:, :], copy).then_inc(ab_ready, 1)

            def high(k, w32, w):
                act.wait_ge(w_scaled, k + 1)
                nc.scalar.activation(w[:, 0], w32, copy).then_inc(w_high, 1)

            def weights(k):
                if k == 0:
                    for c in range(CH):
                        act.wait_ge(wvo_psum, c + 1)
                        nc.scalar.activation(wvo32[:, c, :], banks[c][:, :], copy).then_inc(wvo_ready, 1)
                if k == 9:
                    high(2, wvo32, wvo)
                if k == 10:
                    high(3, ffn32, ffn)

            def Sx(a):
                act.wait_ge(scale_a, a.n // TILES + 1)
                act.wait_ge(x_in_loaded[a.par], (a.half + 1) * 16)
                nc.scalar.activation(x_in[a.par][:, :], x_in[a.par][:, :], copy, scale=sx
                                     ).then_inc(S["x_scaled"], 1)

            def Tx(a):
                act.wait_ge(S["xT_psum"], done(a.n))
                act.wait_ge(S["k_psum"], done(a.n - 2))
                nc.scalar.activation(xT[a.par][:, 0, :], TRANS[:, :], copy).then_inc(S["xTh"], 1)

            def Lk(a):
                act.wait_ge(S["k_psum"], done(a.n))
                if not a.first:
                    act.wait_ge(S["k_shifted"], done(a.n - TILES))
                slot = snapped(act, a.t * D)
                nc.scalar.activation(keys[:, ds(slot, D)], KEYS[:, :], copy).then_inc(S["k_stored"], 1)

            def Lq(a):
                act.wait_ge(S["x_scaled"], done(a.n))
                if not a.first:
                    act.wait_ge(S["g_psum"], done(a.n - TILES))
                slot = snapped(act, a.t * (2 * D))
                nc.scalar.activation(xn[:, ds(slot, D)], x_in[a.par][:, :], copy).then_inc(S["xnh"], 1)
                act.wait_ge(S["q_bias"], done(a.n))
                act.wait_ge(S["pT_psum"], done(a.n - 1))
                act.wait_ge(S["q_recip"], done(a.n - 1))
                nc.scalar.activation(exp_q[:, :], QUERIES[:, :], exp, bias=q_bias_c, scale=kq,
                                     accum_out=q_sum).then_inc(S["q_exp"], 1)

            def TP(a):
                act.wait_ge(S["pT_psum"], done(a.n))
                slot = snapped(act, a.ring * (2 * D))
                nc.scalar.activation(probs[:, ds(slot, D)], P_TRANS[:, :], copy, scale=PS).then_inc(S["pTh"], 1)

            def CB(b):
                act.wait_ge(kmax_row, b + 1)
                nc.scalar.activation(kshift[:, :], MISC[:, :], copy).then_inc(kshift_ready, 1)

            def exponentials(n, par):
                act.wait_ge(S["k_shifted"], done(n))
                nc.scalar.activation(exp_k[par][:, :], exp_k[par][:, :], exp, scale=kk).then_inc(S["k_exp"], 1)

            def E0(b):
                act.wait_ge(scale_b, b + 1)
                exponentials(b * TILES, 0)

            def B(k):
                if not (isinstance(k.t, int) and k.t == TILES - 1):
                    exponentials(k.n + 1, 1 - k.par)

            def GE(b):
                act.wait_ge(S["g_psum"], done(b * TILES + TILES - 1))
                for c in range(CH):
                    nc.scalar.activation(gt[:, 0, c, :], banks[c][:, :], copy, scale=GS).then_inc(gh, 1)

            def M(b, m):
                act.wait_ge(m_sum, b * CH + m + 1)
                nc.scalar.activation(attn[:, 0, m, :], exp_k[m % 2][:, :], copy).then_inc(mh, 1)

            def T1(c):
                act.wait_ge(S["x1T_psum"], done(c.n))
                act.wait_ge(S["ffn_psum"], done(c.n - 2))
                nc.scalar.activation(x1T[c.par][:, 0, :], x1T_bank(c)[:, :], copy, scale=NS).then_inc(S["x1Th"], 1)

            walk(act, {"setup": setup, "weights": weights, "Sx": Sx, "Tx": Tx, "Lk": Lk, "Lq": Lq, "TP": TP,
                       "CB": CB, "E0": E0,
                       "B": B, "GE": GE, "M": M, "T1": T1})

        @block.vector
        def _(dve):
            V = nc.vector

            def power(dst, src, tmp, link):
                link(V.tensor_scalar(tmp, src, 1e-12, 1.0 / TOP, ALU.max, ALU.mult))
                link(V.reciprocal(tmp, tmp))
                link(V.tensor_scalar(dst.bitcast(i32), tmp.bitcast(i32), 0x7F800000, None, ALU.bitwise_and))

            chain = [0]

            def link_set(ins):
                chain[0] += 1
                ins.then_inc(dve_set, 1)
                dve.wait_ge(dve_set, chain[0])

            def absmax_of(k, w):
                return V.tensor_reduce(w_abs[:, k:k + 1], w, AX.XY, ALU.max, apply_absolute_value=True)

            def scale_of(k, src, count=1):
                dst = sw[:, k:k + count]
                power(dst, w_abs_all[:, src:src + count], t01[:, 0:count], link_set)
                return V.reciprocal(isw[:, k:k + count], dst)

            def setup():
                for name in names:
                    dve.sem_inc(S[name], LEAD)
                dve.sem_inc(S["x_absmax"], TILES)
                for k in range(2):
                    dve.sem_inc(out_stored[k], 16)
                dve.sem_inc(leads_set, 1)
                V.memset(absmax_p, 0.0).then_inc(absmax_part, 1)
                link_set(V.memset(kmax[:, :], FAR))
                dve.wait_ge(rows_all, 1)
                link_set(V.tensor_reduce(bo_max, bo_all[:, :], AX.X, ALU.max, apply_absolute_value=True))
                dve.wait_ge(wq_loaded, 16)
                link_set(absmax_of(0, wq32))
                dve.wait_ge(wk_loaded, 16)
                absmax_of(1, wk32).then_inc(w_absmax, 1)
                dve.wait_ge(w_absmax_all, 1)
                scale_of(0, 0, 2).then_inc(w_scale, 1)
                for k in range(TILES // 4):
                    dve.wait_ge(x0_loaded[k], 16)
                    link_set(V.tensor_reduce(absmax_cols[:, k:k + 1], x0[:, k * 4 * D:(k + 1) * 4 * D], AX.X, ALU.max,
                                             apply_absolute_value=True))

            def weights(k):
                big = 1.5 * 2.0 ** 23
                if k == 0:
                    dve.wait_ge(ffn_loaded, 16)
                    absmax_of(4, ffn32).then_inc(w_absmax, 1)
                if k == 1:
                    dve.wait_ge(w_absmax_all, 2)
                    link_set(V.tensor_scalar(t1, w_abs_all[:, 4:5], 1.0 / 7.0, None, ALU.mult))
                    link_set(V.reciprocal(t2, t1))
                    link_set(V.tensor_scalar(ffn32, ffn32, t2, big, ALU.mult, ALU.add))
                if k == 2:
                    link_set(V.tensor_scalar(ffn32, ffn32, big, -8.0, ALU.subtract, ALU.max))
                if k == 3:
                    link_set(V.tensor_scalar(ffn32, ffn32, 7.0, t1, ALU.min, ALU.mult))
                if k == 4:
                    dve.wait_ge(wvo_ready, CH)
                    link_set(absmax_of(2, wvo32))
                if k == 5:
                    dve.wait_ge(ab_ready, CH)
                    link_set(V.tensor_tensor(ffn32, ffn32, ab32, ALU.add))
                if k == 6:
                    dve.wait_ge(consts, 6)
                    for c in range(CH):
                        diag = ffn32[:, c, c * P:(c + 1) * P]
                        link_set(V.tensor_tensor(diag, diag, ident[:, :], ALU.add))
                if k == 7:
                    absmax_of(3, ffn32).then_inc(w_absmax, 1)
                if k == 8:
                    dve.wait_ge(w_absmax_all, 3)
                    scale_of(2, 2, 2).then_inc(w_scale, 1)
                    dve.wait_ge(w_scale, 2)
                    V.tensor_scalar(wvo32, wvo32, sw[:, 2:3], None, ALU.mult).then_inc(w_scaled, 1)
                if k == 9:
                    V.tensor_scalar(ffn32, ffn32, sw[:, 3:4], None, ALU.mult).then_inc(w_scaled, 1)
                    link_set(V.tensor_scalar(b_attn, w_abs_all[:, 2:3], D * ATTN_SCALE, None, ALU.mult))
                    link_set(V.tensor_scalar(k_ffn, isw[:, 3:4], 1.0 / NS, None, ALU.mult))

            def X(x):
                dve.wait_ge(x_abs_loaded[x.q], (x.quad - (TILES // 4 - 1)) * 16)
                V.tensor_reduce(absmax_cols[:, ds(x.t, 1)], x_abs[x.q][:, :], AX.X, ALU.max,
                                apply_absolute_value=True).then_inc(S["x_absmax"], 1)

            def XS(s):
                first = isinstance(s, int) and s == 0
                if not first:
                    dve.wait_ge(S["x_absmax"], done(s * TILES + TILES - 1))
                    dve.wait_ge(absmax_all, s)
                cols = absmax_cols[:, 0:TILES // 4 if first else TILES]
                V.tensor_reduce(absmax_p, cols, AX.X, ALU.max).then_inc(absmax_part, 1)

            def linker(sem_, start):
                at = [start]

                def link(ins):
                    at[0] = at[0] + 1
                    ins.then_inc(sem_, 1)
                    dve.wait_ge(sem_, at[0])
                return link

            def scale_next_(s):
                dve.wait_ge(absmax_all, s + 1)
                link = linker(next_link, s * NEXT_LINKS)
                link(V.tensor_scalar(ax, absmax_new, 1.0, None, ALU.mult))
                power(sx_next, ax, t3, link)
                link(V.reciprocal(isx, sx_next))
                V.tensor_scalar(kq_next, isx, isw[:, 0:1], None, ALU.mult).then_inc(scale_next, 1)

            def turn_a(s):
                dve.wait_ge(scale_next, s + 1)
                dve.wait_ge(S["x_scaled"], done(s * TILES - 1))
                dve.wait_ge(S["q_exp"], done(s * TILES - 1))
                V.tensor_scalar(sx, sx_next, 1.0, None, ALU.mult)
                V.tensor_scalar(kq, kq_next, 1.0, None, ALU.mult).then_inc(scale_a, 1)

            def turn_b(b):
                dve.wait_ge(S["k_exp"], done(b * TILES - 1))
                if not (isinstance(b, int) and b == 0):
                    dve.wait_ge(S["rq_scaled"], done(b * TILES - (TILES + 1)))
                link = linker(turn_link, b * TURN_LINKS)
                link(V.tensor_scalar(kk, isx, isw[:, 1:2], None, ALU.mult))
                link(V.tensor_scalar(t0, ax, b_attn, bo_max, ALU.mult, ALU.add))
                power(s_attn, t0, t1, link)
                link(V.tensor_scalar(t0, s_attn, PS, None, ALU.mult))
                parity = snapped(dve, b % 2)
                link(V.reciprocal(g_attn[:, ds(parity, 1)], t0))
                link(V.tensor_scalar(t0, isx, isw[:, 2:3], ATTN_SCALE / (GS * PS), ALU.mult, ALU.mult))
                link(V.tensor_scalar(f_attn, t0, s_attn, None, ALU.mult))
                V.tensor_scalar(bo_scaled[:, :], bo_all[:, :], s_attn, None, ALU.mult).then_inc(scale_b, 1)

            def Tx(a):
                dve.wait_ge(S["xTh"], done(a.n))
                V.tensor_tensor(xT[a.par][:, 1, :], TRANS[:, :], xT[a.par][:, 0, :], ALU.subtract).then_inc(S["xTl"], 1)

            def Lk(a):
                dve.wait_ge(S["k_stored"], done(a.n))
                dve.wait_ge(S["k_max"], done(a.n - 1))
                if not a.first:
                    dve.wait_ge(kmax_reset, a.n // TILES)
                slot = snapped(dve, a.t * D)
                V.tensor_tensor(kmax[:, :], kmax[:, :], keys[:, ds(slot, D)], ALU.max).then_inc(S["k_max"], 1)

            def Lq(a):
                dve.wait_ge(S["q_psum"], done(a.n))
                V.tensor_reduce(q_rowmax_c, QUERIES[:, :], AX.X, ALU.max, negate=True).then_inc(S["q_rowmax"], 1)
                dve.wait_ge(S["q_rowmax"], done(a.n))
                dve.wait_ge(S["q_exp"], done(a.n - 1))
                V.tensor_scalar(q_bias_c, q_rowmax_c, kq, None, ALU.mult).then_inc(S["q_bias"], 1)

            def TP(a):
                dve.wait_ge(S["q_exp"], done(a.n))
                V.reciprocal(q_recip_all[:, ds(a.n, 1)], q_sum).then_inc(S["q_recip"], 1)
                dve.wait_ge(S["pTh"], done(a.n))
                slot = snapped(dve, a.ring * (2 * D))
                V.scalar_tensor_tensor(probs[:, ds(slot + D, D)], P_TRANS[:, :], PS, probs[:, ds(slot, D)],
                                       ALU.mult, ALU.subtract).then_inc(S["pTl"], 1)

            def CM(b):
                dve.wait_ge(kmaxT, b + 1)
                V.tensor_reduce(kmax_c, TRANS[:, :].rearrange("p (c n) -> p c n", c=CH), AX.X, ALU.max
                                ).then_inc(kmax_col, 1)
                dve.wait_ge(kmax_col, b + 1)
                V.tensor_tensor(exp_k[1][:, :].rearrange("p (c n) -> p c n", c=CH),
                                ones[:, :].unsqueeze(1).to_broadcast([P, CH, P]),
                                kmax_c.unsqueeze(2).to_broadcast([P, CH, P]), ALU.mult).then_inc(kmax_spread, 1)

            def split_e(n, par):
                dve.wait_ge(S["k_exp"], done(n))
                dve.wait_ge(S["g_psum"], done(n - 2))
                V.tensor_scalar(ek[par][:, 0, :], exp_k[par][:, :], PS, None, ALU.mult).then_inc(S["ekh"], 1)
                dve.wait_ge(S["ekh"], done(n))
                V.scalar_tensor_tensor(ek[par][:, 1, :], exp_k[par][:, :], PS, ek[par][:, 0, :],
                                       ALU.mult, ALU.subtract).then_inc(S["ek_split"], 1)

            def E0(b):
                split_e(b * TILES, 0)

            def B(k):
                if not (isinstance(k.t, int) and k.t == TILES - 1):
                    split_e(k.n + 1, 1 - k.par)

            def KS(b):
                dve.wait_ge(ksum_psum, b + 1)
                V.reciprocal(rk, MISC[:, 0:CH]).then_inc(ksum_recip, 1)
                dve.wait_ge(ksum_recip, b + 1)
                V.tensor_scalar(rkf, rk, f_attn, None, ALU.mult).then_inc(ksum_ready, 1)

            def GE(b):
                for c in range(CH):
                    dve.wait_ge(gh, b * CH + c + 1)
                    V.scalar_tensor_tensor(gt[:, 1, c, :], banks[c][:, :], GS, gt[:, 0, c, :],
                                           ALU.mult, ALU.subtract).then_inc(g_split, 1)

            def M(b, m):
                dve.wait_ge(m_psum, b * CH + m + 1)
                dve.wait_ge(ksum_ready, b + 1)
                if m < 2:
                    dve.wait_ge(S["k_summed"], done(b * TILES + TILES - 1))
                else:
                    dve.wait_ge(m_split, b * CH + m - 1)
                V.scalar_tensor_tensor(exp_k[m % 2][:, :], banks[m][:, :], rkf[:, m:m + 1], bo_scaled[:, :],
                                       ALU.mult, ALU.add).then_inc(m_sum, 1)

            def statistics(c, v, which, ln):
                V.bn_stats(stats[:, 2 * which + c.par, 0:6], v).then_inc(S["yz"[which] + "_stats"], 1)
                dve.wait_ge(S["yz"[which] + "_stats"], done(c.n))
                apart(dve)
                V.bn_aggr(stats[:, 2 * which + c.par, 6:8], stats[:, 2 * which + c.par, 0:6]
                          ).then_inc(S[ln + "_stats"], 1)

            def PM(c):
                dve.wait_ge(S["attn_psum"], done(c.n))
                dve.wait_ge(S["rq_scaled"], done(c.n))
                dve.wait_ge(y_loaded[c.q], (c.quad + 1) * 16)
                V.scalar_tensor_tensor(y[c.q][:, :], banks[c.par][:, :], rqg[c.par], y[c.q][:, :],
                                       ALU.mult, ALU.add).then_inc(S["y_sum"], 1)
                dve.wait_ge(S["y_sum"], done(c.n))
                statistics(c, y[c.q][:, :], 0, "ln1")

            def N1(c):
                dve.wait_ge(S["ln1_rstd"], done(c.n))
                V.tensor_scalar(y[c.q][:, :], y[c.q][:, :], stats[:, c.par, 6:7], rstd1[c.par],
                                ALU.subtract, ALU.mult).then_inc(S["x1_ready"], 1)

            def T1(c):
                dve.wait_ge(S["x1Th"], done(c.n))
                V.scalar_tensor_tensor(x1T[c.par][:, 1, :], x1T_bank(c)[:, :], NS, x1T[c.par][:, 0, :],
                                       ALU.mult, ALU.subtract).then_inc(S["x1T_split"], 1)

            def F(c):
                dve.wait_ge(S["ffn_psum"], done(c.n))
                dve.wait_ge(out_stored[c.par], (c.half + 1) * 16)
                V.scalar_tensor_tensor(z[c.par][:, :], ffn_bank(c)[:, :], k_ffn, bias_all[:, :],
                                       ALU.mult, ALU.add).then_inc(S["z_sum"], 1)

            def FS(c):
                dve.wait_ge(S["z_sum"], done(c.n))
                statistics(c, z[c.par][:, :], 1, "ln2")

            def N2(c):
                dve.wait_ge(S["ln2_rstd"], done(c.n))
                V.tensor_scalar(z[c.par][:, :], z[c.par][:, :], stats[:, 2 + c.par, 6:7], rstd2[c.par],
                                ALU.subtract, ALU.mult).then_inc(S["out_ready"], 1)

            walk(dve, {"setup": setup, "weights": weights, "X": X, "XS": XS, "scale_next": scale_next_,
                       "turn_a": turn_a, "turn_b": turn_b, "Tx": Tx,
                       "Lk": Lk, "Lq": Lq, "TP": TP, "CM": CM, "E0": E0, "B": B, "KS": KS, "GE": GE, "M": M, "PM": PM,
                       "N1": N1, "T1": T1, "F": F, "FS": FS, "N2": N2})

        @block.tensor
        def _(pe):
            mm = nc.tensor.matmul

            def chunk(c):
                return slice(c * P, (c + 1) * P)

            def transposes(bank, src):
                for c in range(CH):
                    last = nc.tensor.transpose(bank[:, chunk(c)], src[:, chunk(c)], ident[:, :])
                return last

            def split_product(bank, left, right, before_chunk=None):
                for c in range(CH):
                    if before_chunk is not None:
                        before_chunk(c)
                    mm(bank, left(0, c), right(0, c), start=c == 0, stop=False)
                    mm(bank, left(0, c), right(1, c), start=False, stop=False)
                    last = mm(bank, left(1, c), right(0, c), start=False, stop=c == CH - 1)
                return last

            def setup():
                pe.wait_ge(consts, 6)
                for k, (bank, row, there) in enumerate(((KEYS, bo_row, bo_loaded), (QUERIES, bias_row, bias_loaded))):
                    pe.wait_ge(there, 16)
                    mm(bank[:, :], ones[0:1, :], row, start=True, stop=True).then_inc(rows_psum, 1)
                pe.wait_ge(leads_set, 1)
                pe.wait_ge(wv_loaded, 16)
                for m in range(CH):
                    for c in range(CH):
                        last = nc.tensor.transpose(banks[m][:, chunk(c)], wv32[:, c, chunk(m)], ident[:, :])
                    last.then_inc(wv_psum, 1)
                pe.wait_ge(a_loaded, 16)
                for c in range(CH):
                    last = nc.tensor.transpose(TRANS[0:RANK, chunk(c)], a32[:, c * RANK:(c + 1) * RANK], ident[:, :])
                last.then_inc(aT_psum, 1)
                pe.wait_ge(wo_loaded, 16)
                pe.wait_ge(wvT_ready, CH)
                for c in range(CH):
                    for m in range(CH):
                        last = mm(banks[c][:, :], wvT[:, m, chunk(c)], wo32[:, m, :], start=m == 0, stop=m == CH - 1)
                    last.then_inc(wvo_psum, 1)
                pe.wait_ge(b_loaded, 16)
                pe.wait_ge(aT_ready, 1)
                pe.wait_ge(rows_all, 2)
                for c in range(CH):
                    mm(banks[4 + c][:, :], aT[:, chunk(c)], b32, start=True, stop=True).then_inc(ab_psum, 1)
                pe.wait_ge(ab_ready, CH)
                pe.wait_ge(w_split, 1)

            def Tx(a):
                pe.wait_ge(S["x_scaled"], done(a.n))
                pe.wait_ge(S["xTl"], done(a.n - 1))
                transposes(TRANS, x_in[a.par]).then_inc(S["xT_psum"], 1)

            def from_x(a):
                return lambda part, c: xT[a.par][:, part, chunk(c)]

            def Lk(a):
                pe.wait_ge(S["k_stored"], done(a.n - 1))
                if isinstance(a.n, int) and a.n == 0:
                    pe.wait_ge(w_split, 2)
                split_product(KEYS[:, :], from_x(a), lambda part, c: wk[:, part, c, :]).then_inc(S["k_psum"], 1)

            def Lq(a):
                pe.wait_ge(S["xTl"], done(a.n))
                pe.wait_ge(S["q_exp"], done(a.n - 1))
                split_product(QUERIES[:, :], from_x(a), lambda part, c: wq[:, part, c, :]).then_inc(S["q_psum"], 1)

            def TP(a):
                pe.wait_ge(S["q_exp"], done(a.n))
                pe.wait_ge(S["pTl"], done(a.n - 1))
                if isinstance(a.t, int) and a.t == 7 and not a.first:
                    pe.wait_ge(ksum_recip, a.n // TILES)
                transposes(P_TRANS, exp_q).then_inc(S["pT_psum"], 1)

            def CT(b):
                pe.wait_ge(S["k_max"], done(b * TILES + TILES - 1))
                pe.wait_ge(S["xTl"], done(b * TILES + TILES - 1))
                transposes(TRANS, kmax).then_inc(kmaxT, 1)

            def CB(b):
                pe.wait_ge(kmax_spread, b + 1)
                pe.wait_ge(S["pTl"], done(b * TILES + TILES - 1))
                transposes(MISC, exp_k[1]).then_inc(kmax_row, 1)

            def clear(b):
                pe.wait_ge(wvo_ready, CH)
                pe.wait_ge(S["y_sum"], done(b * TILES - 1))
                pe.wait_ge(S["x1T_split"], done(b * TILES - 1))
                for c in (1, 2, 0, 3):
                    if c in (0, 3):
                        pe.wait_ge(S["z_sum"], done(b * TILES - (2 if c == 0 else 1)))
                    mm(banks[c][:, :], zeros[:, :], wq[:, 0, 0, :], start=True, stop=False)

            def B(k):
                pe.wait_ge(S["ek_split"], done(k.n))
                pe.wait_ge(S["xn_split"], done(k.n))
                slot = snapped(pe, k.t * (2 * D))
                end = isinstance(k.t, int) and k.t == TILES - 1
                for c in range(CH):
                    high = xn[:, ds(slot + c * P, P)]
                    low = xn[:, ds(slot + (D + c * P), P)]
                    mm(banks[c][:, :], high, ek[k.par][:, 0, :], start=False, stop=False)
                    mm(banks[c][:, :], high, ek[k.par][:, 1, :], start=False, stop=False)
                    last = mm(banks[c][:, :], low, ek[k.par][:, 0, :], start=False, stop=end)
                last.then_inc(S["g_psum"], 1)

            def KS(b):
                pe.wait_ge(S["k_summed"], done(b * TILES + TILES - 1))
                pe.wait_ge(S["pTl"], done(BATCHES * TILES - 1 if isinstance(b, int) else (b + 1) * TILES + 6))
                for c in range(CH):
                    last = mm(MISC[:, c:c + 1], ksum[:, chunk(c)], ones[:, 0:1], start=True, stop=True)
                last.then_inc(ksum_psum, 1)

            def M(b, m):
                def chunk_split(c):
                    if m == 0:
                        pe.wait_ge(w_split, 4)
                        pe.wait_ge(g_split, b * CH + c + 1)

                split_product(banks[m][:, :], lambda part, c: gt[:, part, c, chunk(m)],
                              lambda part, c: wvo[:, part, c, :], chunk_split).then_inc(m_psum, 1)

            def PM(c):
                pe.wait_ge(S["pTl"], done(c.n))
                pe.wait_ge(S["y_sum"], done(c.n - 2))

                def chunk_split(k):
                    if isinstance(c.t, int) and c.t == 0:
                        pe.wait_ge(m_split, snapped(pe, c.quad // (TILES // 4) * CH + (k + 1)))

                slot = snapped(pe, c.ring * (2 * D))
                split_product(banks[c.par][:, :], lambda part, k: probs[:, ds(slot + (part * D + k * P), P)],
                              lambda part, k: attn[:, part, k, :], chunk_split).then_inc(S["attn_psum"], 1)

            def T1(c):
                pe.wait_ge(S["x1_ready"], done(c.n))
                if not is_tile(c, TILES - 1):
                    pe.wait_ge(S["x1T_split"], done(c.n - 1))
                transposes(x1T_bank(c), y[c.q]).then_inc(S["x1T_psum"], 1)

            def F(c):
                pe.wait_ge(S["x1T_split"], done(c.n))
                if not is_tile(c, TILES - 2):
                    pe.wait_ge(S["z_sum"], done(c.n - (2 if is_tile(c, TILES - 1) else 1)))
                split_product(ffn_bank(c)[:, :], lambda part, k: x1T[c.par][:, part, chunk(k)],
                              lambda part, k: ffn[:, part, k, :]).then_inc(S["ffn_psum"], 1)

            walk(pe, {"setup": setup, "Tx": Tx, "Lk": Lk, "Lq": Lq, "TP": TP, "CT": CT, "CB": CB, "B": B,
                      "clear": clear, "KS": KS, "M": M, "PM": PM, "T1": T1, "F": F})


_INS = {"x": "L0_attn_x", "Wq": "L0_attn_Wq", "Wk": "L0_attn_Wk", "Wv": "L0_attn_Wv", "Wo": "L0_attn_Wo",
        "bo": "L0_attn_bo", "kernel": "L0_ffn_kernel", "bias": "L0_ffn_bias", "lora_a": "L0_ffn_a",
        "lora_b": "L0_ffn_b"}


def kernel(**inputs):
    import numpy as np
    import concourse.bacc as bacc
    from concourse.bass_utils import run_bass_kernel_spmd

    nc = bacc.Bacc("TRN2", target_bir_lowering=False, num_devices=1, dynamic_dma_scratch_size=4096)
    arrays, args = {}, {}
    for arg, name in _INS.items():
        a = np.ascontiguousarray(inputs[name])
        arrays[f"in_{arg}"] = a
        args[arg] = nc.dram_tensor(f"in_{arg}", a.shape, mybir.dt.from_np(a.dtype), kind="ExternalInput").ap()
    shape = (BATCHES, TOKENS, D)
    args["out"] = nc.dram_tensor("out_dram", shape, mybir.dt.float32, kind="ExternalOutput").ap()
    build(nc, **args)
    r = run_bass_kernel_spmd(nc, [arrays], core_ids=[0])
    return r.results[0]["out_dram"]
```
